# Optimizing a Trainium2 kernel written in Bass

```python
import numpy as np
import jax
import jax.numpy as jnp

def _softmax(x, axis=-1):
    return jax.nn.softmax(x, axis=axis)

def _gelu(x):
    return jax.nn.gelu(x, approximate=True)

def _silu(x):
    return jax.nn.silu(x)

def _sigmoid(x):
    return jax.nn.sigmoid(x)

def _layernorm(x, axis=-1, eps=1e-05):
    m = jnp.mean(x, axis=axis, keepdims=True)
    v = jnp.var(x, axis=axis, keepdims=True)
    return (x - m) / jnp.sqrt(v + eps)

def _scatter_add(tgt, idx, src, axis=0):
    return tgt.at[idx].add(src)

def _segment_sum(src, seg, n):
    return jax.ops.segment_sum(src, seg, n)
kernel_name = 'mk_flamingo_gated_d1_seqx_r8_4bc8f0'

def setup_inputs(seed: int=0):
    np.random.seed(seed)
    _w = jnp.asarray

    def _rec_inputs():
        import jax
        import jax.numpy as jnp
        _rk = jax.random.key(seed)
        x = -0.0003929 + 0.9999 * jax.random.normal(jax.random.fold_in(_rk, 1), (32, 64, 512), jnp.float32)
        _lenS = 64 - jax.random.randint(jax.random.fold_in(_rk, 7), (32,), 0, max(1, 64 // 4) + 1, jnp.int32)
        _lenS2 = 64 - jax.random.randint(jax.random.fold_in(_rk, 8), (32,), 0, max(1, 64 // 4) + 1, jnp.int32)
        _ctx_4096P = jax.random.normal(jax.random.fold_in(_rk, 11), (32, 16, 512), jnp.float32)
        _ctx_4096c = jax.random.dirichlet(jax.random.fold_in(_rk, 511), 0.3 * jnp.ones((16,), jnp.float32), (32, 64))
        _ctx_4096t = jnp.einsum('bsk,bkd->bsd', _ctx_4096c, _ctx_4096P)
        _ctx_4096t = _ctx_4096t * jax.lax.rsqrt(jnp.mean(jnp.square(_ctx_4096t)) + 1e-12) * 0.953939
        ctx_4096 = 2.81802e-05 + 1.00001 * (_ctx_4096t + 0.3 * jax.random.normal(jax.random.fold_in(_rk, 611), (32, 64, 512), jnp.float32))
        _g = jax.random.normal(jax.random.fold_in(_rk, 9001), (2, 1), jnp.float32)
        _g = jnp.sign(_g) * jnp.maximum(jnp.abs(_g), 1.0) + (_g == 0) * 1.0
        g_xattn = _g[0]
        g_ffn = _g[1]
        return (x, ctx_4096, g_xattn, g_ffn)
    x, ctx_4096, g_xattn, g_ffn = _rec_inputs()

    def _L0_xattn_setup():
        import jax, jax.numpy as jnp
        import numpy as np
        DIM = 64
        HEADS = 8
        DIM_HEAD = 64
        HIDDEN = HEADS * DIM_HEAD
        SCALE = DIM_HEAD ** (-0.5)
        key = jax.random.key(seed)
        ks = jax.random.split(key, 9)
        b, n = (8, 512)
        std = 1.0 / np.sqrt(DIM)
        return {'q': jax.random.normal(ks[0], (b, DIM, n), jnp.float32), 'k': jax.random.normal(ks[1], (b, DIM, n), jnp.float32), 'v': jax.random.normal(ks[2], (b, DIM, n), jnp.float32), 'Wq': jax.random.normal(ks[3], (HIDDEN, DIM), jnp.float32) * std, 'Wk': jax.random.normal(ks[4], (HIDDEN, DIM), jnp.float32) * std, 'Wv': jax.random.normal(ks[5], (HIDDEN, DIM), jnp.float32) * std, 'Wo': jax.random.normal(ks[6], (DIM, HIDDEN), jnp.float32) * (1.0 / np.sqrt(HIDDEN)), 'bo': jax.random.normal(ks[7], (DIM,), jnp.float32) * 0.01, 'g': jnp.ones((1, DIM, 1), jnp.float32)}
    _L0_xattn_all = _L0_xattn_setup()
    _L0_xattn_in = {k: v for k, v in _L0_xattn_all.items() if k in ('Wq', 'Wk', 'Wv', 'Wo', 'bo', 'g')}
    del _L0_xattn_all

    def _L0_ffn_setup():
        import jax, jax.numpy as jnp
        import numpy as np
        HIDDEN = 512
        INTER = 1376
        GROUPSIZE = 128
        PACK = 8

        def dequant_gptq(qweight, scales, zeros, groupsize):
            K = qweight.shape[0] * PACK
            N = qweight.shape[1]
            k = jnp.arange(K)
            q = qweight[k // PACK, :] >> (k % PACK * 4)[:, None] & 15
            n = jnp.arange(N)
            z = zeros[:, n // PACK] >> (n % PACK * 4)[None, :] & 15
            s = scales.astype(jnp.float32)
            zp = (z.astype(jnp.float32) + 1.0) * s
            g = k // groupsize
            return q.astype(jnp.float32) * s[g] - zp[g]
        key = jax.random.key(seed)
        ks = jax.random.split(key, 11)
        imax = 2147483647
        G_h = HIDDEN // GROUPSIZE
        G_i = (INTER + GROUPSIZE - 1) // GROUPSIZE
        x = (jax.random.normal(ks[0], (2, 256, HIDDEN), dtype=jnp.float32) * 0.5).astype(jnp.float16)
        return {'x': x, 'gate_qweight': jax.random.randint(ks[1], (HIDDEN // PACK, INTER), 0, imax, dtype=jnp.int32), 'gate_scales': (jax.random.uniform(ks[2], (G_h, INTER), dtype=jnp.float32) * 0.01 + 0.001).astype(jnp.float16), 'gate_zeros': jax.random.randint(ks[3], (G_h, INTER // PACK), 0, imax, dtype=jnp.int32), 'up_qweight': jax.random.randint(ks[4], (HIDDEN // PACK, INTER), 0, imax, dtype=jnp.int32), 'up_scales': (jax.random.uniform(ks[5], (G_h, INTER), dtype=jnp.float32) * 0.01 + 0.001).astype(jnp.float16), 'up_zeros': jax.random.randint(ks[6], (G_h, INTER // PACK), 0, imax, dtype=jnp.int32), 'down_qweight': jax.random.randint(ks[7], (INTER // PACK, HIDDEN), 0, imax, dtype=jnp.int32), 'down_scales': (jax.random.uniform(ks[8], (G_i, HIDDEN), dtype=jnp.float32) * 0.01 + 0.001).astype(jnp.float16), 'down_zeros': jax.random.randint(ks[9], (G_i, HIDDEN // PACK), 0, imax, dtype=jnp.int32)}
    _L0_ffn_all = _L0_ffn_setup()
    _L0_ffn_in = {k: v for k, v in _L0_ffn_all.items() if k in ('gate_qweight', 'gate_scales', 'gate_zeros', 'up_qweight', 'up_scales', 'up_zeros', 'down_qweight', 'down_scales', 'down_zeros')}
    del _L0_ffn_all
    return {'x': x, 'ctx_4096': ctx_4096, 'g_xattn': g_xattn, 'g_ffn': g_ffn, 'L0_xattn_Wq': _L0_xattn_in['Wq'], 'L0_xattn_Wk': _L0_xattn_in['Wk'], 'L0_xattn_Wv': _L0_xattn_in['Wv'], 'L0_xattn_Wo': _L0_xattn_in['Wo'], 'L0_xattn_bo': _L0_xattn_in['bo'], 'L0_xattn_g': _L0_xattn_in['g'], 'L0_ffn_gate_qweight': _L0_ffn_in['gate_qweight'], 'L0_ffn_gate_scales': _L0_ffn_in['gate_scales'], 'L0_ffn_gate_zeros': _L0_ffn_in['gate_zeros'], 'L0_ffn_up_qweight': _L0_ffn_in['up_qweight'], 'L0_ffn_up_scales': _L0_ffn_in['up_scales'], 'L0_ffn_up_zeros': _L0_ffn_in['up_zeros'], 'L0_ffn_down_qweight': _L0_ffn_in['down_qweight'], 'L0_ffn_down_scales': _L0_ffn_in['down_scales'], 'L0_ffn_down_zeros': _L0_ffn_in['down_zeros']}

def reference(x, ctx_4096, g_xattn, g_ffn, L0_xattn_Wq, L0_xattn_Wk, L0_xattn_Wv, L0_xattn_Wo, L0_xattn_bo, L0_xattn_g, L0_ffn_gate_qweight, L0_ffn_gate_scales, L0_ffn_gate_zeros, L0_ffn_up_qweight, L0_ffn_up_scales, L0_ffn_up_zeros, L0_ffn_down_qweight, L0_ffn_down_scales, L0_ffn_down_zeros):
    import jax
    import jax.numpy as jnp

    def _L0_xattn_ref(q, k, v, Wq, Wk, Wv, Wo, bo, g):
        import jax, jax.numpy as jnp
        import numpy as np
        DIM = 64
        HEADS = 8
        DIM_HEAD = 64
        HIDDEN = HEADS * DIM_HEAD
        SCALE = DIM_HEAD ** (-0.5)
        b = q.shape[0]
        qh = jnp.einsum('bcn,oc->bon', q, Wq).reshape(b, HEADS, DIM_HEAD, -1)
        kh = jnp.einsum('bcn,oc->bon', k, Wk).reshape(b, HEADS, DIM_HEAD, -1)
        vh = jnp.einsum('bcn,oc->bon', v, Wv).reshape(b, HEADS, DIM_HEAD, -1)
        qh = jax.nn.softmax(qh, axis=-2) * SCALE
        kh = jax.nn.softmax(kh, axis=-1)
        context = jnp.einsum('bhdn,bhen->bhde', kh, vh)
        out = jnp.einsum('bhde,bhdn->bhen', context, qh)
        out = out.reshape(b, HIDDEN, -1)
        out = jnp.einsum('bcn,oc->bon', out, Wo) + bo[None, :, None]
        norm = jnp.maximum(jnp.sqrt(jnp.sum(out * out, axis=1, keepdims=True)), 1e-12)
        return out / norm * g * np.sqrt(DIM)

    def _L0_ffn_ref(x, gate_qweight, gate_scales, gate_zeros, up_qweight, up_scales, up_zeros, down_qweight, down_scales, down_zeros):
        import jax, jax.numpy as jnp
        import numpy as np
        HIDDEN = 512
        INTER = 1376
        GROUPSIZE = 128
        PACK = 8

        def dequant_gptq(qweight, scales, zeros, groupsize):
            K = qweight.shape[0] * PACK
            N = qweight.shape[1]
            k = jnp.arange(K)
            q = qweight[k // PACK, :] >> (k % PACK * 4)[:, None] & 15
            n = jnp.arange(N)
            z = zeros[:, n // PACK] >> (n % PACK * 4)[None, :] & 15
            s = scales.astype(jnp.float32)
            zp = (z.astype(jnp.float32) + 1.0) * s
            g = k // groupsize
            return q.astype(jnp.float32) * s[g] - zp[g]
        B, S, H = x.shape
        x2 = x.reshape(-1, H).astype(jnp.float32)
        Wg = dequant_gptq(gate_qweight, gate_scales, gate_zeros, GROUPSIZE)
        Wu = dequant_gptq(up_qweight, up_scales, up_zeros, GROUPSIZE)
        Wd = dequant_gptq(down_qweight, down_scales, down_zeros, GROUPSIZE)
        gate = x2 @ Wg
        up = x2 @ Wu
        inter = gate * jax.nn.sigmoid(gate) * up
        out = (inter @ Wd).astype(jnp.float16)
        return out.reshape(B, S, H)
    x = x + jnp.tanh(g_xattn[0]) * _L0_xattn_ref(_layernorm(x, axis=-1), ctx_4096, ctx_4096, L0_xattn_Wq, L0_xattn_Wk, L0_xattn_Wv, L0_xattn_Wo, L0_xattn_bo, L0_xattn_g)
    x = x + jnp.tanh(g_ffn[0]) * _L0_ffn_ref(_layernorm(x, axis=-1), L0_ffn_gate_qweight, L0_ffn_gate_scales, L0_ffn_gate_zeros, L0_ffn_up_qweight, L0_ffn_up_scales, L0_ffn_up_zeros, L0_ffn_down_qweight, L0_ffn_down_scales, L0_ffn_down_zeros)
    return x

_drawn_inputs = setup_inputs


def setup_inputs(seed=0):
    import zlib

    import numpy as np

    out = dict(_drawn_inputs(seed))
    spreads = {'L0_xattn_g': (1.0, 0.2)}
    factors = {}
    for name, (base, spread) in spreads.items():
        noise = np.random.default_rng([zlib.crc32(name.encode()), seed]).standard_normal(out[name].shape)
        drawn = base * np.exp(spread * noise) if base else spread * noise
        out[name] = jnp.asarray(drawn.astype(out[name].dtype))
    for name, factor in factors.items():
        out[name] = (out[name] * factor).astype(out[name].dtype)
    return out
```

```python
from contextlib import ExitStack

import concourse.bass as bass
from concourse import mybir

F32, F32R, BF16, F16, I32 = (mybir.dt.float32, mybir.dt.float32r, mybir.dt.bfloat16, mybir.dt.float16,
                             mybir.dt.int32)
ALU = mybir.AluOpType
ACT = mybir.ActivationFunctionType
AX = mybir.AxisListType

P = 128
BATCH, C, N = 32, 64, 512
HEADS, DH = 8, 64
O = HEADS * DH
OT = O // P
NT = N // P
PAIRS = BATCH // 2
EPS = 1e-5
INTER, GROUP, PACK = 1376, 128, 8
GH = N // GROUP
IT = (INTER + P - 1) // P
ROWS = BATCH * C
CHUNK = 512
CHUNKS = ROWS // CHUNK
TPC = CHUNK // P
XSCALE = 256.0


CONSTS_MADE = 26
WEIGHT_DMAS = 12


def width(it):
    return min(P, INTER - it * P)


def moments(pool, stats, work, inv_counts, half_eps, minus_half, step, before):
    count = [0]

    def tt(out, a, b, op):
        ins = pool.tensor_tensor(out, a, b, op)
        count[0] += 1
        if count[0] <= 7:
            ins.then_inc(step, 1)
            pool.wait_ge(step, before + count[0])
        return ins

    tt(work[..., 2:4], stats[..., 1:3], stats[..., 4:6], ALU.add)
    tt(work[..., 0:2], work[..., 2:4], inv_counts, ALU.mult)
    tt(work[..., 4:5], stats[..., 1:2], stats[..., 4:5], ALU.subtract)
    tt(work[..., 5:6], work[..., 4:5], half_eps[..., 0:1], ALU.mult)
    tt(work[..., 4:5], work[..., 5:6], work[..., 5:6], ALU.mult)
    tt(work[..., 5:6], work[..., 4:5], work[..., 1:2], ALU.add)
    tt(work[..., 6:7], work[..., 5:6], half_eps[..., 1:2], ALU.add)
    return tt(work[..., 7:8], work[..., 6:7], minus_half, ALU.pow)


def attention(nc, x, ctx, g_xattn, wq, wk, wv, wo, bo, g, xall, stats2):
    with ExitStack() as st:
        def sb(name, shape, dt=F32):
            return st.enter_context(nc.sbuf_tensor(name, shape, dt))

        def sem(name):
            return st.enter_context(nc.semaphore(name))

        ident = sb("ident", [P, P])
        wq_sb = sb("wq_sb", [P, OT, 2, C])
        wk_sb = sb("wk_sb", [P, OT, 2, C])
        wv_sb = sb("wv_sb", [P, OT, 2, C])
        wo_sb = sb("wo_sb", [C, O])
        wqT_hi, wqT_lo = sb("wqT_hi", [P, O], F32R), sb("wqT_lo", [P, O], F32R)
        wkT_hi, wkT_lo = sb("wkT_hi", [P, O], F32R), sb("wkT_lo", [P, O], F32R)
        woT = sb("woT", [P, OT, C])
        foldT = sb("foldT", [P, 2, HEADS, C])
        head_of_row = sb("head_of_row", [P, 2 * OT, P])
        spread = sb("spread", [P, 2 * OT, P], F32R)
        minus_spread = sb("minus_spread", [P, 2 * OT, P], F32R)
        head_sum = sb("head_sum", [P, 2, 32])
        batch_sum = sb("batch_sum", [P, 32])
        minus_half = sb("minus_half", [P, 8])
        ones = sb("ones", [P, 8])
        inv_counts, half_eps = sb("inv_counts", [P, 2]), sb("half_eps", [P, 2])
        bo_col, gate_col, g_col, tanh_col = (sb(n, [P, 1]) for n in ("bo_col", "gate_col", "g_col", "tanh_col"))

        ctx_raw = sb("ctx_raw", [P, 2, N])
        xn = sb("xn", [P, N])
        xs = sb("xs", [P, 2, 2, N], F32R)
        cs = sb("cs", [P, 2, N], F32R)
        stats = sb("stats", [P, 6])
        ln_work = sb("ln_work", [P, 8])
        qmax = sb("qmax", [P, NT, 2, HEADS])
        qmax_rows = sb("qmax_rows", [P, N], F32R)
        kneg = sb("kneg", [P, 2 * OT])
        ksum = sb("ksum", [P, 2 * OT])
        kinv = sb("kinv", [P, 2, 2 * OT])
        ek = sb("ek", [P, 2, OT, N])
        ekT = sb("ekT", [P, 2, NT, O])
        eq = sb("eq", [P, 2, 2, OT, N])
        ctxT = sb("ctxT", [P, NT, P])
        den = sb("den", [P, N])
        den_sq = sb("den_sq", [P, C])
        rden = sb("rden", [P, C])
        rden_parts = sb("rden_parts", [P, 2, C], F32R)
        rden_rows = sb("rden_rows", [P, N], F32R)
        kctxT = sb("kctxT", [P, O])
        fold = sb("fold", [P, 2 * OT, C])
        y0 = sb("y0", [P, N])
        ysq = sb("ysq", [P, N])
        ss_rows = sb("ss_rows", [32, N])
        ss_sq = sb("ss_sq", [P, 8])
        ss_max = sb("ss_max", [P, 8])
        rn_sq = sb("rn_sq", [P, 8])
        rn_parts = sb("rn_parts", [P, 2, 8], F32R)
        rn_rows = sb("rn_rows", [P, N], F32R)
        batch_of_row = sb("batch_of_row", [P, P])
        spread_batch = sb("spread_batch", [P, P], F32R)
        yn = sb("yn", [P, N])

        bank = [st.enter_context(nc.psum_tensor(f"bank{i}", [P, 512], F32)) for i in range(8)]
        dve_ring = bank[0:2]
        k_ring = bank[2:4]
        act_ring = bank[4:6]
        small = bank[6:8]

        weights_in, consts_made, weights_T, wT_ready, fold_mm, fold_ready = (
            sem(n) for n in ("weights_in", "consts_made", "weights_T", "wT_ready", "fold_mm", "fold_ready"))
        gate_parts = sem("gate_parts")
        wT_hi_ready, wT_lo_ready = sem("wT_hi_ready"), sem("wT_lo_ready")
        rden_step, norm_step, ss_bounded, bn2_done, yn_ready, rn_mm = (
            sem(n) for n in ("rden_step", "norm_step", "ss_bounded", "bn2_done", "yn_ready", "rn_mm"))
        loaded = [sem("loaded_even"), sem("loaded_odd")]
        ln_stats, pool_step, rstd_ready, xn_ready = (
            sem(n) for n in ("ln_stats", "pool_step", "rstd_ready", "xn_ready"))
        x_hi, x_lo, c_hi, c_lo = (sem(n) for n in ("x_hi", "x_lo", "c_hi", "c_lo"))
        t_mm, k_mm, q_mm, kt_mm, b_mm = (sem(n) for n in ("t_mm", "k_mm", "q_mm", "kt_mm", "b_mm"))
        t_max, k_max, k_exp, kt_evac, q_exp, q_norm = (
            sem(n) for n in ("t_max", "k_max", "k_exp", "kt_evac", "q_exp", "q_norm"))
        d_mm, a_mm, m_mm, qmaxT_mm, ct_mm, f_mm, ss_mm = (
            sem(n) for n in ("d_mm", "a_mm", "m_mm", "qmaxT_mm", "ct_mm", "f_mm", "ss_mm"))
        d_evac, a_evac, m_evac, qmaxT_evac, ct_evac, y_evac, ss_evac = (
            sem(n) for n in ("d_evac", "a_evac", "m_evac", "qmaxT_evac", "ct_evac", "y_evac", "ss_evac"))
        kinv_ready, rden_ready, rn_ready, x1_done = (
            sem(n) for n in ("kinv_ready", "rden_ready", "rn_ready", "x1_done"))
        den_spread, rden_gathered, ss_spread, rn_gathered = (
            sem(n) for n in ("den_spread", "rden_gathered", "ss_spread", "rn_gathered"))

        block = st.enter_context(nc.Block())

        x_rows = x.rearrange("(p two) c n -> p (two c) n", two=2)
        ctx_rows = ctx.rearrange("(p two) c n -> p (two c) n", two=2)

        def masks_made(eng):
            eng.wait_ge(consts_made, CONSTS_MADE)

        @block.sync
        def _(sp):
            def load(p, half, par):
                sp.dma_start(xall[:, p, :], x_rows[p]).then_inc(loaded[par], 16)
                sp.dma_start(ctx_raw[:, par, :], ctx_rows[p]).then_inc(loaded[par], 16)

            def row(ap):
                return ap.rearrange("(c one) -> c one", one=1)

            for w, dst in ((wq, wq_sb), (wk, wk_sb), (wv, wv_sb)):
                for twice in range(2):
                    sp.dma_start(dst[:, :, twice, :], w.rearrange("(t p) c -> p t c", p=P)).then_inc(weights_in, 16)
            sp.dma_start(wo_sb[:, :], wo).then_inc(weights_in, 16)
            load(0, 0, 0)
            load(1, 0, 1)
            for b in range(2):
                half = slice(b * C, (b + 1) * C)
                sp.dma_start(bo_col[half, :], row(bo)).then_inc(weights_in, 16)
                sp.dma_start(g_col[half, :], g.rearrange("one c two -> (one c) two")).then_inc(weights_in, 16)
            sp.dma_start(tanh_col[:, :], row(g_xattn).to_broadcast([P, 1])).then_inc(weights_in, 16)

            def step(p, i, par, project, combine, residual):
                if residual:
                    r2 = p - 2
                    sp.wait_ge(ss_evac, r2 + 1)
                    sp.dma_start(ss_sq[:, :],
                                 ss_rows[0:2, :].rearrange("b (k m) -> b k m", m=8)).then_inc(ss_spread, 16)
                    sp.wait_ge(rn_ready, 2 * r2 + 2)
                    for part in range(2):
                        sp.dma_start(rn_rows[2 * part:2 * part + 2, :].bitcast(F32).rearrange("b (k m) -> b k m", m=8),
                                     rn_parts[:, part, :].bitcast(F32)).then_inc(rn_gathered, 16)
                if combine:
                    r = p - 1
                    sp.wait_ge(d_evac, r + 1)
                    for grp in range(4):
                        sp.dma_start(den_sq[32 * grp:32 * grp + 32, :],
                                     den[32 * grp:32 * grp + 4, :].rearrange("h (k m) -> h k m", m=C)
                                     ).then_inc(den_spread, 16)
                if combine:
                    sp.wait_ge(rden_ready, r + 1)
                    for part in range(2):
                        sp.dma_start(rden_rows[16 * part:16 * part + 16, :].bitcast(F32).rearrange("r (k m) -> r k m", m=C),
                                     rden_parts[:, part, :].bitcast(F32)).then_inc(rden_gathered, 16)

            def step_and_load(p, i, par, project, combine, residual):
                step(p, i, par, project, combine, residual)
                sp.wait_ge(ct_mm, p + 1)
                load(p + 2, i + 1, par)

            step_and_load(0, 0, 0, True, False, False)
            step_and_load(1, 0, 1, True, True, False)
            with sp.Fori(1, PAIRS // 2 - 1) as i:
                step_and_load(2 * i, i, 0, True, True, True)
                step_and_load(2 * i + 1, i, 1, True, True, True)
            step(PAIRS - 2, 0, 0, True, True, True)
            step(PAIRS - 1, 0, 1, True, True, True)
            step(PAIRS, 0, 0, False, True, True)
            step(PAIRS + 1, 0, 1, False, False, True)

        @block.gpsimd
        def _(pool):
            made = [0]

            def then(ins):
                made[0] += 1
                ins.then_inc(consts_made, 1)
                pool.wait_ge(consts_made, made[0])

            then(pool.memset(ident[:, :], 0.0))
            then(pool.memset(head_of_row[:, :, :], 0.0))
            then(pool.memset(head_sum[:, :, :], 0.0))
            then(pool.memset(foldT[:, :, :, :], 0.0))
            then(pool.memset(batch_sum[:, :], 0.0))
            then(pool.memset(minus_half[:, :], -0.5))
            then(pool.memset(ones[:, :], 1.0))
            then(pool.memset(inv_counts[:, 0:1], 0.5))
            then(pool.memset(inv_counts[:, 1:2], 1.0 / N))
            then(pool.memset(half_eps[:, 0:1], 0.5))
            then(pool.memset(half_eps[:, 1:2], EPS))
            then(pool.memset(qmax_rows[:, :].bitcast(F32), 0.0))
            then(pool.memset(rden_rows[:, :].bitcast(F32), 0.0))
            then(pool.memset(rn_rows[:, :].bitcast(F32), 0.0))
            then(pool.memset(batch_of_row[:, :], 0.0))
            then(pool.affine_select(out=ident[:, :], in_=ident[:, :], compare_op=ALU.not_equal, fill=1.0, base=0,
                                    pattern=[[-1, P]], channel_multiplier=1))
            rows = head_of_row[:, :, :].rearrange("r bt (e d) -> r bt e d", e=2)
            for part in range(2):
                then(pool.affine_select(out=rows, in_=rows, compare_op=ALU.not_equal, fill=1.0, base=-16 * part,
                                        pattern=[[-2, 2 * OT], [-1, 2], [0, DH]], channel_multiplier=1))
            rows = batch_of_row[:, :].rearrange("r (b c) -> r b c", b=2)
            for part in range(2):
                then(pool.affine_select(out=rows, in_=rows, compare_op=ALU.not_equal, fill=1.0, base=-2 * part,
                                        pattern=[[-1, 2], [0, C]], channel_multiplier=1))
            for e in range(2):
                half = slice(e * DH, (e + 1) * DH)
                for tt in range(2):
                    then(pool.memset(head_sum[half, tt, :].rearrange("o (m f) -> o m f", f=4)[:, :, 2 * tt + e],
                                     float(DH) ** 0.5))
                then(pool.memset(batch_sum[half, :].rearrange("o (m f) -> o m f", f=2)[:, :, e], 1.0))
            assert made[0] == CONSTS_MADE

            def layernorm(p):
                pool.wait_ge(ln_stats, p + 1)
                moments(pool, stats[:, :], ln_work[:, :], inv_counts[:, :], half_eps[:, :], minus_half[:, 0:1], pool_step, 7 * p).then_inc(rstd_ready, 1)

            def inverse_norm(r):
                pool.wait_ge(ss_bounded, r + 1)
                pool.tensor_tensor(rn_sq[:, :], ss_max[:, :], minus_half[:, :], ALU.pow).then_inc(norm_step, 1)
                pool.wait_ge(norm_step, r + 1)
                pool.tensor_tensor(rn_parts[:, 0, :], rn_sq[:, :], ones[:, :], ALU.mult).then_inc(rn_ready, 1)
                pool.wait_ge(rn_ready, 2 * r + 1)
                pool.tensor_tensor(rn_parts[:, 1, :], rn_sq[:, :], rn_parts[:, 0, :].bitcast(F32),
                                   ALU.subtract).then_inc(rn_ready, 1)

            pool.wait_ge(consts_made, made[0])
            layernorm(0)
            layernorm(1)
            layernorm(2)
            with pool.Fori(2, PAIRS - 1) as p:
                inverse_norm(p - 2)
                layernorm(p + 1)
            inverse_norm(PAIRS - 3)
            inverse_norm(PAIRS - 2)
            inverse_norm(PAIRS - 1)

        def k_slot(b, t):
            return b * OT + t

        @block.scalar
        def _(act):
            act.wait_ge(weights_T, 1)
            act.activation(wqT_hi[:, :], bank[0][:, :], ACT.Copy).then_inc(wT_hi_ready, 1)
            act.wait_ge(weights_T, 2)
            act.activation(wkT_hi[:, :], bank[1][:, :], ACT.Copy, scale=-1.0).then_inc(wT_hi_ready, 1)
            act.wait_ge(weights_T, 3)
            act.activation(woT[:, :, :].rearrange("p t c -> p (t c)"), bank[2][:, 0:OT * C], ACT.Copy).then_inc(wT_ready, 1)
            act.wait_ge(consts_made, CONSTS_MADE)
            act.activation(spread[:, :, :], head_of_row[:, :, :], ACT.Copy).then_inc(wT_ready, 1)
            act.activation(spread_batch[:, :], batch_of_row[:, :], ACT.Copy).then_inc(wT_ready, 1)
            act.activation(minus_spread[:, :, :], head_of_row[:, :, :], ACT.Copy, scale=-1.0).then_inc(wT_ready, 1)
            act.wait_ge(fold_mm, 1)
            for b in range(2):
                rows = slice(b * C, (b + 1) * C)
                for e in range(2):
                    act.activation(foldT[rows, b, e::2, :], bank[3 + e][rows, :].rearrange("c (h d) -> c h d", d=C)[:, e::2, :],
                                   ACT.Copy).then_inc(fold_ready, 1)
            act.wait_ge(weights_in, 16 * WEIGHT_DMAS)
            act.activation(tanh_col[:, :], tanh_col[:, :], ACT.Tanh).then_inc(gate_parts, 1)

            def ctx_high(p, half, par):
                act.wait_ge(loaded[par], 32 * (half + 1))
                for b in range(2):
                    rows = slice(b * C, (b + 1) * C)
                    act.activation(cs[rows, b, :], ctx_raw[rows, par, :], ACT.Copy).then_inc(c_hi, 1)

            def x_high(p, par):
                act.wait_ge(xn_ready, p + 1)
                for b in range(2):
                    rows = slice(b * C, (b + 1) * C)
                    act.activation(xs[rows, par, b, :], xn[rows, :], ACT.Copy).then_inc(x_hi, 1)

            ctx_high(0, 0, 0)
            x_high(0, 0)

            def step(p, i, par, project, combine, residual, last=False):
                r = p - 1

                def k_exps(b):
                    for t in range(OT):
                        n = 8 * p + b * OT + t
                        act.wait_ge(k_max, n + 1)
                        if t == 0 and not first:
                            act.wait_ge(kt_mm, 8 * p - 4 + 4 * b)
                            if b == 0:
                                act.wait_ge(kinv_ready, p)
                        act.activation(ek[:, b, t, :], k_ring[t % 2][:, :], ACT.Exp, bias=kneg[:, k_slot(b, t):k_slot(b, t) + 1],
                                       scale=-1.0, accum_out=ksum[:, k_slot(b, t):k_slot(b, t) + 1]).then_inc(k_exp, 1)

                first = isinstance(p, int) and p == 0
                if project:
                    k_exps(0)
                if combine:
                    act.wait_ge(d_mm, r + 1)
                    act.activation(den[:, :], small[0][:, :], ACT.Copy).then_inc(d_evac, 1)
                if project:
                    k_exps(1)
                if combine:
                    act.wait_ge(a_mm, r + 1)
                    act.activation(kctxT[:, :], small[1][:, :], ACT.Copy).then_inc(a_evac, 1)
                if project:
                    act.wait_ge(qmaxT_mm, p + 1)
                    act.activation(qmax_rows[0:16, :], small[0][0:16, :], ACT.Copy).then_inc(qmaxT_evac, 1)
                    if not last:
                        act.wait_ge(k_mm, 8 * p + 8)
                        ctx_high(p + 1, i + par, 1 - par)
                    for b in range(2):
                        for t in range(NT):
                            act.wait_ge(kt_mm, 8 * p + 4 * b + t + 1)
                            act.activation(ekT[:, b, t, :], act_ring[t % 2][:, :], ACT.Copy).then_inc(kt_evac, 1)
                        if b == 1 and not last:
                            x_high(p + 1, 1 - par)
                        for t in range(OT):
                            act.wait_ge(q_mm, 8 * p + 4 * b + t + 1)
                            act.activation(eq[:, par, b, t, :], act_ring[t % 2][:, :], ACT.Exp).then_inc(q_exp, 1)
                    act.wait_ge(ct_mm, p + 1)
                    act.activation(ctxT[:, :, :].rearrange("n t c -> n (t c)"), small[0][:, :], ACT.Copy).then_inc(ct_evac, 1)
                if combine:
                    act.wait_ge(f_mm, r + 1)
                    if residual:
                        act.wait_ge(yn_ready, r)
                    act.activation(y0[:, :], small[1][:, :], ACT.Identity, bias=bo_col[:, 0:1]).then_inc(y_evac, 1)
                    act.activation(ysq[:, :], small[1][:, :], ACT.Square, bias=bo_col[:, 0:1]).then_inc(y_evac, 1)
                    act.wait_ge(ss_mm, r + 1)
                    act.activation(ss_rows[:, :], small[0][0:32, :], ACT.Copy).then_inc(ss_evac, 1)

            step(0, 0, 0, True, False, False)
            step(1, 0, 1, True, True, False)
            with act.Fori(1, PAIRS // 2 - 1) as i:
                step(2 * i, i, 0, True, True, True)
                step(2 * i + 1, i, 1, True, True, True)
            step(PAIRS - 2, PAIRS // 2 - 1, 0, True, True, True)
            step(PAIRS - 1, PAIRS // 2 - 1, 1, True, True, True, last=True)
            step(PAIRS, PAIRS // 2, 0, False, True, True)

        @block.tensor
        def _(pe):
            pe.wait_ge(consts_made, CONSTS_MADE)
            pe.wait_ge(weights_in, 16 * WEIGHT_DMAS)
            for w, ps in ((wq_sb, bank[0]), (wk_sb, bank[1])):
                for t in range(OT):
                    last = pe.transpose(ps[:, t * P:(t + 1) * P], w[:, t, :, :].rearrange("p a c -> p (a c)"), ident[:, :])
                last.then_inc(weights_T, 1)
            for t in range(OT):
                last = pe.transpose(bank[2][:, t * C:(t + 1) * C], wo_sb[:, t * P:(t + 1) * P], ident[0:C, 0:C])
            last.then_inc(weights_T, 1)
            pe.wait_ge(wT_ready, 1)
            for h in range(HEADS):
                rows = slice((h % 2) * DH, (h % 2 + 1) * DH)
                last = pe.matmul(bank[3 + h % 2][:, h * C:(h + 1) * C], wv_sb[rows, h // 2, :, :].rearrange("p a c -> p (a c)"),
                                 woT[rows, h // 2, :], start=True, stop=True)
            last.then_inc(fold_mm, 1)
            pe.wait_ge(wT_ready, 4)
            pe.wait_ge(wT_lo_ready, 2)
            pe.wait_ge(fold_ready, 4)

            def step(p, i, par, project, combine, residual):
                r = p - 1
                first = isinstance(p, int) and p == 0
                qpar = 1 - par

                def t_and_k(b):
                    for t in range(4):
                        n = 8 * p + 4 * b + t
                        if b == 0 and t < 2:
                            if combine:
                                if residual:
                                    pe.wait_ge(q_norm, 8 * r - 1 + t)
                        else:
                            pe.wait_ge(t_max, n - 1)
                        if t == 0:
                            pe.wait_ge(x_lo, 2 * p + b + 1)
                        pe.matmul(dve_ring[t % 2][:, :], xs[:, par, b, t * P:(t + 1) * P], wqT_hi[:, :],
                                  start=True, stop=True).then_inc(t_mm, 1)
                        if not (first and b == 0 and t < 2):
                            pe.wait_ge(k_exp, n - 1)
                        if t == 0:
                            pe.wait_ge(c_lo, 2 * p + b + 1)
                        pe.matmul(k_ring[t % 2][:, :], wkT_hi[:, t * P:(t + 1) * P], cs[:, b, :], start=True, stop=False)
                        pe.matmul(k_ring[t % 2][:, :], wkT_lo[:, t * P:(t + 1) * P], cs[:, b, :],
                                  start=False, stop=True).then_inc(k_mm, 1)

                def denominators():
                    pe.wait_ge(q_exp, 8 * r + 8)
                    if residual:
                        pe.wait_ge(ss_evac, r)
                    else:
                        pe.wait_ge(ct_evac, r + 1)
                    for tt in range(2):
                        for grp in range(4):
                            b, t = grp // 2, 2 * (grp % 2) + tt
                            last = pe.matmul(small[0][32 * grp:32 * grp + 32, :], head_sum[:, tt, :], eq[:, qpar, b, t, :],
                                             start=(tt == 0), stop=(tt == 1))
                    last.then_inc(d_mm, 1)

                def context():
                    pe.wait_ge(kt_evac, 8 * r + 8)
                    pe.wait_ge(ct_evac, r + 1)
                    if residual:
                        pe.wait_ge(y_evac, 2 * r)
                    for t in range(NT):
                        for b in range(2):
                            last = pe.matmul(small[1][b * C:(b + 1) * C, :], ctxT[:, t, b * C:(b + 1) * C], ekT[:, b, t, :],
                                             start=(t == 0), stop=(t == NT - 1))
                    last.then_inc(a_mm, 1)

                def q_max_rows():
                    pe.wait_ge(t_max, 8 * p + 8)
                    if combine:
                        pe.wait_ge(d_evac, r + 1)
                    for t in range(NT):
                        last = pe.transpose(small[0][0:16, t * P:(t + 1) * P],
                                            qmax[:, t, :, :].rearrange("n b h -> n (b h)"), ident[:, :])
                    last.then_inc(qmaxT_mm, 1)

                def act_ring_free(kind, b, t):
                    if t >= 2:
                        pe.wait_ge(kt_evac if kind == "kt" else q_exp, 8 * p + 4 * b + t - 1)
                    elif kind == "q":
                        pe.wait_ge(kt_evac, 8 * p + 4 * b + t + 3)
                    elif b == 1:
                        pe.wait_ge(q_exp, 8 * p + t + 3)
                    elif not first:
                        pe.wait_ge(q_exp, 8 * p - 1 + t)

                def k_transposed(b, t):
                    act_ring_free("kt", b, t)
                    if t == 0:
                        pe.wait_ge(k_exp, 8 * p + 4 * b + 4)
                    for ot in range(OT):
                        last = pe.transpose(act_ring[t % 2][:, ot * P:(ot + 1) * P], ek[:, b, ot, t * P:(t + 1) * P], ident[:, :])
                    last.then_inc(kt_mm, 1)

                def q_logits(b, t):
                    act_ring_free("q", b, t)
                    if b == 0 and t == 0:
                        pe.wait_ge(qmaxT_evac, p + 1)
                    out, cols = act_ring[t % 2][:, :], slice(t * P, (t + 1) * P)
                    pe.matmul(out, wqT_hi[:, cols], xs[:, par, b, :], start=True, stop=False)
                    pe.matmul(out, wqT_lo[:, cols], xs[:, par, b, :], start=False, stop=False)
                    pe.matmul(out, minus_spread[:, k_slot(b, t), :], qmax_rows[:, :], start=False,
                              stop=True).then_inc(q_mm, 1)

                def fold_context():
                    pe.wait_ge(a_evac, r + 1)
                    for b in range(2):
                        for t in range(OT):
                            for e in range(2):
                                last = pe.matmul(small[1][e * DH:(e + 1) * DH, k_slot(b, t) * C:(k_slot(b, t) + 1) * C],
                                                 kctxT[:, t * P + e * DH:t * P + (e + 1) * DH],
                                                 foldT[:, b, 2 * t + e, :], start=True, stop=True)
                    last.then_inc(m_mm, 1)

                def spread_reciprocals(b, t):
                    n = 8 * r + 4 * b + t
                    if b == 0 and t == 0:
                        pe.wait_ge(rden_gathered, 32 * (r + 1))
                    if b == 0 and t < 2:
                        if project:
                            pe.wait_ge(t_max, 8 * p + 8)
                        else:
                            pe.wait_ge(q_norm, n - 1)
                    else:
                        pe.wait_ge(q_norm, n - 1)
                    pe.matmul(dve_ring[t % 2][:, :], spread[:, k_slot(b, t), :], rden_rows[:, :],
                              start=True, stop=True).then_inc(b_mm, 1)

                def ctx_transposed():
                    pe.wait_ge(loaded[par], 32 * (i + 1))
                    pe.wait_ge(qmaxT_evac, p + 1)
                    for t in range(NT):
                        last = pe.transpose(small[0][:, t * P:(t + 1) * P], ctx_raw[:, par, t * P:(t + 1) * P], ident[:, :])
                    last.then_inc(ct_mm, 1)

                def spread_inverse_norm():
                    pe.wait_ge(rn_gathered, 32 * (r - 1) + 32)
                    if combine:
                        pe.wait_ge(m_evac, r + 1)
                    else:
                        pe.wait_ge(y_evac, 2 * r)
                    pe.matmul(small[1][:, :], spread_batch[:, :], rn_rows[:, :], start=True, stop=True).then_inc(rn_mm, 1)

                def output():
                    pe.wait_ge(q_norm, 8 * r + 8)
                    pe.wait_ge(m_evac, r + 1)
                    if residual:
                        pe.wait_ge(yn_ready, r)
                    for t in range(OT):
                        for b in range(2):
                            last = pe.matmul(small[1][b * C:(b + 1) * C, :], fold[:, k_slot(b, t), :], eq[:, qpar, b, t, :],
                                             start=(t == 0), stop=(t == OT - 1))
                    last.then_inc(f_mm, 1)

                def squared_norms():
                    pe.wait_ge(y_evac, 2 * r + 2)
                    if project:
                        pe.wait_ge(ct_evac, p + 1)
                    else:
                        pe.wait_ge(d_evac, r + 1)
                    pe.matmul(small[0][0:32, :], batch_sum[:, :], ysq[:, :], start=True, stop=True).then_inc(ss_mm, 1)

                if project:
                    t_and_k(0)
                if combine:
                    denominators()
                if project:
                    t_and_k(1)
                if combine:
                    context()
                if project:
                    q_max_rows()
                    for t in range(NT):
                        k_transposed(0, t)
                if combine:
                    fold_context()
                for t in range(OT):
                    if project:
                        q_logits(0, t)
                for b in range(2):
                    for t in range(OT):
                        if combine:
                            spread_reciprocals(b, t)
                        if project:
                            if b == 0:
                                k_transposed(1, t)
                            else:
                                q_logits(1, t)
                    if residual and b == 0:
                        spread_inverse_norm()
                if project:
                    ctx_transposed()
                if combine:
                    output()
                    squared_norms()

            step(0, 0, 0, True, False, False)
            step(1, 0, 1, True, True, False)
            with pe.Fori(1, PAIRS // 2) as i:
                step(2 * i, i, 0, True, True, True)
                step(2 * i + 1, i, 1, True, True, True)
            step(PAIRS, PAIRS // 2, 0, False, True, True)
            step(PAIRS + 1, PAIRS // 2, 1, False, False, True)

        @block.vector
        def _(dve):
            for n, (ps, hi, lo, sign) in enumerate(((bank[0], wqT_hi, wqT_lo, 1.0), (bank[1], wkT_hi, wkT_lo, -1.0))):
                dve.wait_ge(wT_hi_ready, n + 1)
                dve.scalar_tensor_tensor(out=lo[:, :], in0=ps[:, :], scalar=sign, in1=hi[:, :].bitcast(F32), op0=ALU.mult,
                                         op1=ALU.subtract).then_inc(wT_lo_ready, 1)
            dve.wait_ge(gate_parts, 1)
            dve.tensor_scalar(gate_col[:, :], g_col[:, :], tanh_col[:, 0:1], float(C) ** 0.5, ALU.mult,
                              ALU.mult).then_inc(gate_parts, 1)

            dve.wait_ge(gate_parts, 2)

            def layernorm_stats(p, half, par):
                masks_made(dve)
                dve.wait_ge(loaded[par], 32 * (half + 1))
                if not (isinstance(p, int) and p == 0):
                    dve.wait_ge(rstd_ready, p)
                dve.bn_stats(stats[:, :], xall[:, p, :]).then_inc(ln_stats, 1)

            def layernorm_apply(p):
                dve.wait_ge(rstd_ready, p + 1)
                dve.tensor_scalar(xn[:, :], xall[:, p, :], ln_work[:, 0:1], ln_work[:, 7:8], ALU.subtract,
                                  ALU.mult).then_inc(xn_ready, 1)

            def low_part(b, hi_ready, count, raw, split, lo_ready):
                rows, other = slice(b * C, (b + 1) * C), slice((1 - b) * C, (2 - b) * C)
                dve.wait_ge(hi_ready, count)
                dve.tensor_tensor(split[other], raw[rows], split[rows].bitcast(F32), ALU.subtract).then_inc(lo_ready, 1)

            def x_low(p, par):
                dve.wait_ge(xn_ready, p + 1)
                for b in range(2):
                    low_part(b, x_hi, 2 * p + b + 1, xn[:, :], xs[:, par, b, :], x_lo)

            def ctx_low(p, par):
                for b in range(2):
                    low_part(b, c_hi, 2 * p + b + 1, ctx_raw[:, par, :], cs[:, b, :], c_lo)

            layernorm_stats(0, 0, 0)
            ctx_low(0, 0)
            layernorm_apply(0)
            x_low(0, 0)

            def step(p, i, par, project, combine, residual, last=False):
                r, r2 = p - 1, p - 2

                def maxima(b):
                    for t in range(4):
                        n = 8 * p + 4 * b + t
                        dve.wait_ge(t_mm, n + 1)
                        dve.tensor_reduce(qmax[:, t, b, :], dve_ring[t % 2][:, :].rearrange("n (h d) -> n h d", d=DH),
                                          AX.X, ALU.max).then_inc(t_max, 1)
                        dve.wait_ge(k_mm, n + 1)
                        dve.tensor_reduce(kneg[:, k_slot(b, t):k_slot(b, t) + 1], k_ring[t % 2][:, :], AX.X,
                                          ALU.min).then_inc(k_max, 1)

                def normalise(b):
                    for t in range(OT):
                        n = 8 * r + 4 * b + t
                        dve.wait_ge(b_mm, n + 1)
                        e = eq[:, 1 - par, b, t, :]
                        dve.tensor_tensor(e, e, dve_ring[t % 2][:, :], ALU.mult).then_inc(q_norm, 1)

                if project:
                    maxima(0)
                if residual:
                    dve.wait_ge(ss_spread, 16 * (r2 + 1))
                    dve.tensor_scalar(ss_max[:, :], ss_sq[:, :], 1e-24, None, ALU.max).then_inc(ss_bounded, 1)
                if project:
                    if not last:
                        layernorm_stats(p + 1, i + par, 1 - par)
                    maxima(1)
                if combine:
                    dve.wait_ge(den_spread, 64 * (r + 1))
                    dve.reciprocal(rden[:, :], den_sq[:, :]).then_inc(rden_step, 1)
                    dve.wait_ge(rden_step, 2 * r + 1)
                    if residual:
                        dve.wait_ge(rden_gathered, 32 * r)
                    dve.tensor_copy(rden_parts[:, 0, :], rden[:, :]).then_inc(rden_step, 1)
                    dve.wait_ge(rden_step, 2 * r + 2)
                    dve.tensor_tensor(rden_parts[:, 1, :], rden[:, :], rden_parts[:, 0, :].bitcast(F32),
                                      ALU.subtract).then_inc(rden_ready, 1)
                if project and not last:
                    layernorm_apply(p + 1)
                    ctx_low(p + 1, 1 - par)
                if combine:
                    dve.wait_ge(m_mm, r + 1)
                    dve.wait_ge(kinv_ready, r + 1)
                    dve.tensor_tensor(fold[:, :, :], small[1][:, :].rearrange("o (s c) -> o s c", c=C),
                                      kinv[:, 1 - par, :].unsqueeze(2).to_broadcast([P, 2 * OT, C]),
                                      ALU.mult).then_inc(m_evac, 1)
                if combine:
                    normalise(0)
                if residual:
                    dve.wait_ge(rn_mm, r2 + 1)
                    dve.wait_ge(y_evac, 2 * (r2 + 1))
                    dve.tensor_tensor(yn[:, :], y0[:, :], small[1][:, :], ALU.mult).then_inc(yn_ready, 1)
                    dve.wait_ge(yn_ready, r2 + 1)
                    dve.scalar_tensor_tensor(out=xall[:, r2, :], in0=yn[:, :], scalar=gate_col[:, 0:1],
                                             in1=xall[:, r2, :], op0=ALU.mult, op1=ALU.add).then_inc(x1_done, 1)
                if residual:
                    masks_made(dve)
                    dve.wait_ge(x1_done, r2 + 1)
                    dve.bn_stats(stats2[:, r2, :], xall[:, r2, :]).then_inc(bn2_done, 1)
                if project and not last:
                    x_low(p + 1, 1 - par)
                if combine:
                    normalise(1)
                if project:
                    dve.wait_ge(k_exp, 8 * p + 8)
                    dve.reciprocal(kinv[:, par, :], ksum[:, :]).then_inc(kinv_ready, 1)

            step(0, 0, 0, True, False, False)
            step(1, 0, 1, True, True, False)
            with dve.Fori(1, PAIRS // 2 - 1) as i:
                step(2 * i, i, 0, True, True, True)
                step(2 * i + 1, i, 1, True, True, True)
            step(PAIRS - 2, PAIRS // 2 - 1, 0, True, True, True)
            step(PAIRS - 1, PAIRS // 2 - 1, 1, True, True, True, last=True)
            step(PAIRS, PAIRS // 2, 0, False, True, True)
            step(PAIRS + 1, PAIRS // 2, 1, False, False, True)
            dve.wait_ge(bn2_done, PAIRS)


def feed_forward(nc, xall, stats2, g_ffn, gate, up, down, out):
    with ExitStack() as st:
        def sb(name, shape, dt=F32):
            return st.enter_context(nc.sbuf_tensor(name, shape, dt))

        def sem(name):
            return st.enter_context(nc.semaphore(name))

        ident = sb("ident2", [P, P])
        lane = sb("lane", [P, 1], I32)
        nibble = sb("nibble", [P, 1], I32)
        minus_half = sb("minus_half2", [P, PAIRS])
        w_gu = sb("w_gu", [P, 2, GH, INTER], BF16)
        wd_hi, wd_lo = sb("wd_hi", [P, IT, N], F32R), sb("wd_lo", [P, IT, N], F32R)
        packed = sb("packed", [P, 2, INTER], I32)
        ZW = 2 * INTER
        zero = sb("zero", [P, ZW], I32)
        zero_packed = sb("zero_packed", [P, 2, ZW // PACK], I32)
        d_scale = sb("d_scale", [P, 2, N], F16)
        d_int = sb("d_int", [P, N])
        d_w = sb("d_w", [P, 2, N])
        s_rows16 = sb("s_rows16", [2 * GH, INTER], F16)
        scale_T = sb("scale_T", [P, IT, 2 * GH])
        ln_work = sb("ln_work2", [P, PAIRS, 8])
        rstd = sb("rstd2", [P, PAIRS])
        inv_counts, half_eps = sb("inv_counts2", [P, PAIRS, 2]), sb("half_eps2", [P, PAIRS, 2])
        xn = sb("xn2", [P, 2, N])
        xT_hi, xT_lo = sb("xT_hi", [P, GH, ROWS], F16), sb("xT_lo", [P, GH, ROWS], F16)
        tanh_col = sb("tanh_col2", [P, 1])
        acc = sb("acc", [P, 3, 2, CHUNK])
        s_rows = acc[0:2 * GH, :, :, :].rearrange("p a b c -> p (a b c)")[:, 0:INTER]
        sig = sb("sig", [P, CHUNK])
        act_gate = sb("act_gate", [P, CHUNK])
        inter = sb("inter", [P, CHUNK])
        in_hi, in_lo = sb("in_hi", [P, 3, CHUNK], F32R), sb("in_lo", [P, 3, CHUNK], F32R)
        y16 = sb("y16", [P, TPC, N], F16)

        bank = [st.enter_context(nc.psum_tensor(f"ffn_bank{i}", [P, 512], F32)) for i in range(8)]
        y_bank = bank[0:4]
        gu_bank = bank[4:8]

        small_in, made, zero_in = sem("small_in"), sem("made"), [sem("zero_in0"), sem("zero_in1")]
        packed_in, d_scale_in = [sem("packed_in0"), sem("packed_in1")], [sem("d_scale_in0"), sem("d_scale_in1")]
        s_cast, sT_mm, sT_ready, tanh_ready = sem("s_cast"), sem("sT_mm"), sem("sT_ready"), sem("tanh_ready")
        zero_ready, nib, w_int, d_scaled, d_hi, d_lo = (
            sem(n) for n in ("zero_ready", "nib", "w_int", "d_scaled", "d_hi", "d_lo"))
        rstd_step, xn_ready, xT_mm, xT_hi_ready, xT_lo_ready = (
            sem(n) for n in ("rstd_step", "xn2_ready", "xT_mm", "xT_hi_ready", "xT_lo_ready"))
        gu_mm, s0_done, acc_done, sig_ready, gs_ready, inter_ready, in_hi_ready, in_lo_ready, down_mm = (
            sem(n) for n in ("gu_mm", "s0_done", "acc_done", "sig_ready", "gs_ready", "inter_ready", "in_hi_ready",
                             "in_lo_ready", "down_mm"))
        y16_ready, out_ready, stored = sem("y16_ready"), sem("out_ready"), sem("stored")

        zero_parts = [(0, 0, 2), (0, 2, 2), (1, 0, 2), (1, 2, 2), (2, 0, 4), (2, 4, 4), (2, 8, 3)]
        columns = (INTER, INTER, N)
        groups = [(m, k, n) for n, (m, first, count) in enumerate(zero_parts) for k in range(first, first + count)]
        matrices = (gate, up, down)

        block = st.enter_context(nc.Block())

        def last_unit(j, it, first):
            if it:
                return j, it - 1, first
            return None if first else (j - 1, IT - 1, isinstance(j, int) and j == 1)

        def two_units_back(j, it, first):
            return last_unit(*last_unit(j, it, first))

        def projected(j, it, first=None):
            return (IT - 1 + TPC) * j + (it + 1 if it < IT - 1 else it + TPC)

        def rows_of(m, k):
            return width(k) if m == 2 else P

        @block.sync
        def _(sp):
            sp.dma_start(s_rows16[0:GH, :], gate[1]).then_inc(small_in, 16)
            sp.dma_start(s_rows16[GH:2 * GH, :], up[1]).then_inc(small_in, 16)
            sp.dma_start(tanh_col[:, :], g_ffn.rearrange("(c one) -> c one", one=1).to_broadcast([P, 1])).then_inc(small_in, 16)
            done = 0
            downs = 0
            for n, (m, first, count) in enumerate(zero_parts):
                words = columns[m] // PACK
                if n >= 2:
                    sp.wait_ge(zero_ready, n - 1)
                sp.dma_start(zero_packed[:, n % 2, 0:count * words],
                             matrices[m][2][first:first + count, :].rearrange("g w -> (g w)").partition_broadcast(P)
                             ).then_inc(zero_in[n % 2], 16)
                for k in range(first, first + count):
                    if done >= 2:
                        sp.wait_ge(w_int, done - 1)
                    rows = rows_of(m, k)
                    words_k = matrices[m][0][k * GROUP // PACK:(k * GROUP + rows) // PACK, :]
                    sp.dma_start(packed[0:rows, done % 2, 0:columns[m]],
                                 words_k.unsqueeze(1).to_broadcast([rows // PACK, PACK, columns[m]])
                                 ).then_inc(packed_in[done % 2], 16)
                    if m == 2:
                        if downs >= 2:
                            sp.wait_ge(d_scaled, downs - 1)
                        sp.dma_start(d_scale[:, downs % 2, :],
                                     down[1][k:k + 1, :].rearrange("g w -> (g w)").partition_broadcast(P)
                                     ).then_inc(d_scale_in[downs % 2], 16)
                        downs += 1
                    done += 1

            out_rows = out.rearrange("(p two) c n -> p (two c) n", two=2)
            with sp.Fori(0, PAIRS) as tile:
                sp.wait_ge(out_ready, tile + 1)
                sp.dma_start(out_rows[tile], xall[:, tile, :]).then_inc(stored, 16)
            sp.wait_ge(stored, 16 * PAIRS)

        @block.gpsimd
        def _(pool):
            pool.memset(ident[:, :], 0.0).then_inc(made, 1)
            pool.memset(minus_half[:, :], -0.5).then_inc(made, 1)
            pool.iota(lane[:, :], [[0, 1]], base=0, channel_multiplier=4).then_inc(made, 1)
            pool.wait_ge(made, 3)
            pool.affine_select(out=ident[:, :], in_=ident[:, :], compare_op=ALU.not_equal, fill=1.0, base=0,
                               pattern=[[-1, P]], channel_multiplier=1).then_inc(made, 1)
            for col, (t, value) in enumerate(((inv_counts, 0.5), (inv_counts, 1.0 / N), (half_eps, 0.5), (half_eps, EPS))):
                pool.memset(t[:, :, col % 2], value).then_inc(made, 1)
            pool.wait_ge(made, 8)
            moments(pool, stats2[:, :, :], ln_work[:, :, :], inv_counts[:, :, :], half_eps[:, :, :], minus_half[:, :].unsqueeze(2), rstd_step,
                    0).then_inc(rstd_step, 1)
            pool.wait_ge(rstd_step, 8)
            pool.tensor_scalar(rstd[:, :], ln_work[:, :, 7], XSCALE, None, ALU.mult).then_inc(rstd_step, 1)

            def low_part(j, it, first):
                n, w = IT * j + it, width(it)
                pool.wait_ge(in_hi_ready, n + 1)
                if not (first and it < 2):
                    pool.wait_ge(down_mm, projected(*two_units_back(j, it, first)))
                pool.tensor_tensor(in_lo[0:w, it % 3, :], inter[0:w, :], in_hi[0:w, it % 3, :].bitcast(F32),
                                   ALU.subtract).then_inc(in_lo_ready, 1)

            for it in range(IT):
                low_part(0, it, True)
            with pool.Fori(1, CHUNKS) as j:
                for it in range(IT):
                    low_part(j, it, False)

        @block.scalar
        def _(act):
            act.wait_ge(small_in, 48)
            act.activation(tanh_col[:, :], tanh_col[:, :], ACT.Tanh).then_inc(tanh_ready, 1)
            act.activation(s_rows, s_rows16[:, :], ACT.Copy, scale=1.0 / XSCALE).then_inc(s_cast, 1)
            act.wait_ge(sT_mm, 1)
            act.activation(scale_T[:, 0:IT - 1, :].rearrange("p i s -> p (i s)"), bank[4][:, 0:(IT - 1) * 8], ACT.Copy).then_inc(sT_ready, 1)
            act.activation(scale_T[0:width(IT - 1), IT - 1, :], bank[4][0:width(IT - 1), (IT - 1) * 8:IT * 8], ACT.Copy).then_inc(sT_ready, 1)
            for tile in range(PAIRS):
                act.wait_ge(xT_mm, tile + 1)
                act.activation(xT_hi[:, :, tile * P:(tile + 1) * P], bank[tile % 2][:, :].rearrange("k (g r) -> k g r", g=GH),
                               ACT.Copy).then_inc(xT_hi_ready, 1)
            for k in range(IT):
                act.wait_ge(d_scaled, k + 1)
                act.activation(wd_hi[0:width(k), k, :], d_w[0:width(k), k % 2, :], ACT.Copy).then_inc(d_hi, 1)

            def open_sum(j, it, m, first):
                n, w = IT * j + it, width(it)
                act.wait_ge(gu_mm, 8 * n + m + 1)
                if not (first and it < 2):
                    act.wait_ge(inter_ready, n - 1)
                act.activation(acc[0:w, it % 3, m, :], gu_bank[m][0:w, :], ACT.Copy,
                               scale=scale_T[0:w, it, 4 * m:4 * m + 1]).then_inc(s0_done, 1)

            def sigmoid(j, it, first):
                n, w = IT * j + it, width(it)
                act.wait_ge(acc_done, 6 * n + 5)
                if not (first and it == 0):
                    act.wait_ge(gs_ready, n)
                act.activation(sig[0:w, :], acc[0:w, it % 3, 0, :], ACT.Sigmoid).then_inc(sig_ready, 1)

            def high_part(j, it, first):
                n, w = IT * j + it, width(it)
                act.wait_ge(inter_ready, n + 1)
                if not (first and it < 2):
                    act.wait_ge(down_mm, projected(*two_units_back(j, it, first)))
                act.activation(in_hi[0:w, it % 3, :], inter[0:w, :], ACT.Copy).then_inc(in_hi_ready, 1)

            def half_precision(j, t):
                act.wait_ge(down_mm, projected(j, IT - 1) - TPC + t + 1)
                act.activation(y16[:, t, :], y_bank[t][:, :], ACT.Copy).then_inc(y16_ready, 1)

            def chunk(j, first):
                for it in range(IT):
                    before = last_unit(j, it, first)
                    evacuate = not first and it == 1
                    if before:
                        sigmoid(*before)
                    if it == 2 and not first:
                        half_precision(j - 1, 3)
                    open_sum(j, it, 0, first)
                    if evacuate:
                        half_precision(j - 1, 0)
                    open_sum(j, it, 1, first)
                    if evacuate:
                        half_precision(j - 1, 1)
                    if before:
                        high_part(*before)
                    if evacuate:
                        half_precision(j - 1, 2)
                    if it == IT - 1 and not first:
                        act.wait_ge(out_ready, TPC * j)

            chunk(0, True)
            with act.Fori(1, CHUNKS) as j:
                chunk(j, False)
            sigmoid(CHUNKS - 1, IT - 1, False)
            high_part(CHUNKS - 1, IT - 1, False)
            for t in range(TPC):
                half_precision(CHUNKS - 1, t)

        @block.tensor
        def _(pe):
            pe.wait_ge(made, 4)
            pe.wait_ge(s_cast, 1)
            for it in range(IT):
                w = width(it)
                last = pe.transpose(bank[4][0:w, it * 8:(it + 1) * 8], s_rows[:, it * P:it * P + w], ident[0:8, 0:8])
            last.then_inc(sT_mm, 1)
            for tile in range(PAIRS):
                pe.wait_ge(xn_ready, tile + 1)
                if tile >= 2:
                    pe.wait_ge(xT_lo_ready, tile - 1)
                for g in range(GH):
                    last = pe.transpose(bank[tile % 2][:, g * P:(g + 1) * P], xn[:, tile % 2, g * P:(g + 1) * P], ident[:, :])
                last.then_inc(xT_mm, 1)
            pe.wait_ge(sT_ready, 2)
            pe.wait_ge(xT_lo_ready, PAIRS)
            pe.wait_ge(w_int, 2 * GH)

            def gate_up(j, it, job, first):
                n, w, (g, m) = IT * j + it, width(it), divmod(job, 2)
                if job < 4:
                    if not (first and it == 0):
                        pe.wait_ge(acc_done, 6 * n - 3 + job)
                elif job < 6:
                    pe.wait_ge(s0_done, 2 * n + job - 3)
                else:
                    pe.wait_ge(acc_done, 6 * n + job - 5)
                lhsT = w_gu[:, m, g, it * P:it * P + w]
                rows = bass.ds(j * CHUNK, CHUNK)
                pe.matmul(gu_bank[job % 4][0:w, :], lhsT, xT_hi[:, g, rows], start=True, stop=False)
                pe.matmul(gu_bank[job % 4][0:w, :], lhsT, xT_lo[:, g, rows], start=False, stop=True).then_inc(gu_mm, 1)

            def down_product(j, it, first, k):
                n, w, buf = IT * j + it, width(it), it % 3
                kind, t = divmod(k, TPC) if it < IT - 1 else (k % 3, k // 3)
                if k == 0:
                    pe.wait_ge(in_hi_ready, n + 1)
                    if first:
                        pe.wait_ge(d_lo, it + 1)
                if it == 0 and not first and kind == 0:
                    pe.wait_ge(y16_ready, TPC * (j - 1) + t + 1)
                if kind == 2 and t == 0:
                    pe.wait_ge(in_lo_ready, n + 1)
                left = (in_hi, in_hi, in_lo)[kind][0:w, buf, t * P:(t + 1) * P]
                right = (wd_hi, wd_lo, wd_hi)[kind][0:w, it, :]
                ins = pe.matmul(y_bank[t][:, :], left, right, start=(it == 0 and kind == 0), stop=(it == IT - 1 and kind == 2))
                if k == 11 or it == IT - 1 and kind == 2:
                    ins.then_inc(down_mm, 1)

            def chunk(j, first):
                for it in range(IT):
                    before = last_unit(j, it, first)
                    before = before and last_unit(*before)
                    k = 0
                    for job in range(8):
                        gate_up(j, it, job, first)
                        while before and k < 12 * (job + 1) // 8:
                            down_product(*before, k)
                            k += 1

            chunk(0, True)
            with pe.Fori(1, CHUNKS) as j:
                chunk(j, False)
            for it in (IT - 2, IT - 1):
                for k in range(12):
                    down_product(CHUNKS - 1, it, False, k)

        @block.vector
        def _(dve):
            dve.wait_ge(made, 4)
            dve.tensor_scalar(nibble[:, :], lane[:, :], 31, None, ALU.bitwise_and).then_inc(nib, 1)
            dve.wait_ge(rstd_step, 9)
            for tile in range(PAIRS):
                if tile >= 2:
                    dve.wait_ge(xT_mm, tile - 1)
                dve.tensor_scalar(xn[:, tile % 2, :], xall[:, tile, :], ln_work[:, tile, 0:1], rstd[:, tile:tile + 1],
                                  ALU.subtract, ALU.mult).then_inc(xn_ready, 1)
                dve.wait_ge(xT_hi_ready, tile + 1)
                cols = slice(tile * P, (tile + 1) * P)
                dve.tensor_tensor(xT_lo[:, :, cols], bank[tile % 2][:, :].rearrange("k (g r) -> k g r", g=GH),
                                  xT_hi[:, :, cols], ALU.subtract).then_inc(xT_lo_ready, 1)
            dve.wait_ge(nib, 1)
            done = 0
            for n, (m, first_group, count) in enumerate(zero_parts):
                words = columns[m] // PACK
                dve.wait_ge(zero_in[n % 2], 16 * (n // 2 + 1))
                if done:
                    dve.wait_ge(w_int, done)
                for e in range(PACK):
                    last = dve.tensor_scalar(zero[:, 0:count * columns[m]].rearrange("p (w e) -> p w e", e=PACK)[:, :, e],
                                             zero_packed[:, n % 2, 0:count * words], 4 * e, 15,
                                             ALU.logical_shift_right, ALU.bitwise_and)
                last.then_inc(zero_ready, 1)
                for k in range(first_group, first_group + count):
                    rows, cols = rows_of(m, k), columns[m]
                    word = packed[0:rows, done % 2, 0:cols]
                    dve.wait_ge(packed_in[done % 2], 16 * (done // 2 + 1))
                    dve.tensor_scalar(word, word, nibble[0:rows, 0:1], 15, ALU.logical_shift_right,
                                      ALU.bitwise_and).then_inc(nib, 1)
                    dve.wait_ge(nib, done + 2)
                    dve.wait_ge(zero_ready, n + 1)
                    z = zero[0:rows, (k - first_group) * cols:(k - first_group + 1) * cols]
                    if m == 2:
                        dve.scalar_tensor_tensor(out=d_int[0:rows, :], in0=word, scalar=1.0, in1=z, op0=ALU.subtract,
                                                 op1=ALU.subtract).then_inc(w_int, 1)
                        dve.wait_ge(w_int, done + 1)
                        dve.wait_ge(d_scale_in[k % 2], 16 * (k // 2 + 1))
                        if k >= 2:
                            dve.wait_ge(d_hi, k - 1)
                        dve.tensor_tensor(d_w[0:rows, k % 2, :], d_int[0:rows, :], d_scale[0:rows, k % 2, :],
                                          ALU.mult).then_inc(d_scaled, 1)
                        dve.wait_ge(d_hi, k + 1)
                        dve.tensor_tensor(wd_lo[0:rows, k, :], d_w[0:rows, k % 2, :], wd_hi[0:rows, k, :].bitcast(F32),
                                          ALU.subtract).then_inc(d_lo, 1)
                    else:
                        dve.scalar_tensor_tensor(out=w_gu[:, m, k, :], in0=word, scalar=1.0, in1=z, op0=ALU.subtract,
                                                 op1=ALU.subtract).then_inc(w_int, 1)
                    done += 1
            dve.wait_ge(tanh_ready, 1)
            dve.wait_ge(sT_ready, 2)

            def add_group(j, it, job):
                n, w, (g, m) = IT * j + it, width(it), divmod(job, 2)
                dve.wait_ge(gu_mm, 8 * n + job + 1)
                if g == 1:
                    dve.wait_ge(s0_done, 2 * n + m + 1)
                else:
                    dve.wait_ge(acc_done, 6 * n + job - 3)
                dve.scalar_tensor_tensor(out=acc[0:w, it % 3, m, :], in0=gu_bank[job % 4][0:w, :],
                                         scalar=scale_T[0:w, it, 4 * m + g:4 * m + g + 1], in1=acc[0:w, it % 3, m, :],
                                         op0=ALU.mult, op1=ALU.add).then_inc(acc_done, 1)

            def activated(j, it, first):
                n, w, buf = IT * j + it, width(it), it % 3
                dve.wait_ge(sig_ready, n + 1)
                if not (first and it == 0):
                    dve.wait_ge(inter_ready, n)
                dve.tensor_tensor(act_gate[0:w, :], acc[0:w, buf, 0, :], sig[0:w, :], ALU.mult).then_inc(gs_ready, 1)
                dve.wait_ge(gs_ready, n + 1)
                dve.wait_ge(acc_done, 6 * n + 6)
                if not (first and it == 0):
                    dve.wait_ge(in_lo_ready, n)
                dve.tensor_tensor(inter[0:w, :], act_gate[0:w, :], acc[0:w, buf, 1, :],
                                  ALU.mult).then_inc(inter_ready, 1)

            def residual(j, t):
                tile = TPC * j + t
                dve.wait_ge(y16_ready, tile + 1)
                dve.scalar_tensor_tensor(out=xall[:, tile, :], in0=y16[:, t, :], scalar=tanh_col[:, 0:1],
                                         in1=xall[:, tile, :], op0=ALU.mult, op1=ALU.add).then_inc(out_ready, 1)

            def chunk(j, first):
                for it in range(IT):
                    before = last_unit(j, it, first)
                    if before:
                        activated(*before)
                    for job in range(2, 8):
                        add_group(j, it, job)
                    if 3 <= it < 3 + TPC and not first:
                        residual(j - 1, it - 3)

            chunk(0, True)
            with dve.Fori(1, CHUNKS) as j:
                chunk(j, False)
            activated(CHUNKS - 1, IT - 1, False)
            for t in range(TPC):
                residual(CHUNKS - 1, t)


_INS = ["x", "ctx_4096", "g_xattn", "g_ffn", "L0_xattn_Wq", "L0_xattn_Wk", "L0_xattn_Wv", "L0_xattn_Wo", "L0_xattn_bo",
        "L0_xattn_g", "L0_ffn_gate_qweight", "L0_ffn_gate_scales", "L0_ffn_gate_zeros", "L0_ffn_up_qweight",
        "L0_ffn_up_scales", "L0_ffn_up_zeros", "L0_ffn_down_qweight", "L0_ffn_down_scales", "L0_ffn_down_zeros"]


def build(nc, x, ctx, g_xattn, g_ffn, wq, wk, wv, wo, bo, g, gate_q, gate_s, gate_z, up_q, up_s, up_z, down_q, down_s,
          down_z, out):
    with ExitStack() as st:
        xall = st.enter_context(nc.sbuf_tensor("xall", [P, PAIRS, N], F32))
        stats2 = st.enter_context(nc.sbuf_tensor("stats2", [P, PAIRS, 6], F32))
        attention(nc, x, ctx, g_xattn, wq, wk, wv, wo, bo, g, xall, stats2)
        feed_forward(nc, xall, stats2, g_ffn, (gate_q, gate_s, gate_z), (up_q, up_s, up_z), (down_q, down_s, down_z), out)


def kernel(**inputs):
    import numpy as np
    import concourse.bacc as bacc
    from concourse.bass_utils import run_bass_kernel_spmd

    nc = bacc.Bacc("TRN2", target_bir_lowering=False, num_devices=1)
    arrays, args = {}, []
    for name in _INS:
        a = np.ascontiguousarray(inputs[name])
        arrays[f"in_{name}"] = a
        args.append(nc.dram_tensor(f"in_{name}", a.shape, mybir.dt.from_np(a.dtype), kind="ExternalInput").ap())
    out = nc.dram_tensor("out_x", (BATCH, C, N), F32, kind="ExternalOutput").ap()
    build(nc, *args, out)
    return run_bass_kernel_spmd(nc, [arrays], core_ids=[0]).results[0]["out_x"]
```

```python
from contextlib import ExitStack

import concourse.bass as bass
from concourse import mybir

F32, F32R, BF16, F16, I32 = (mybir.dt.float32, mybir.dt.float32r, mybir.dt.bfloat16, mybir.dt.float16,
                             mybir.dt.int32)
ALU = mybir.AluOpType
ACT = mybir.ActivationFunctionType
AX = mybir.AxisListType

P = 128
BATCH, C, N = 32, 64, 512
HEADS, DH = 8, 64
O = HEADS * DH
OT = O // P
NT = N // P
PAIRS = BATCH // 2
EPS = 1e-5
INTER, GROUP, PACK = 1376, 128, 8
GH = N // GROUP
IT = (INTER + P - 1) // P
ROWS = BATCH * C
CHUNK = 512
CHUNKS = ROWS // CHUNK
TPC = CHUNK // P
XSCALE = 256.0


CONSTS_MADE = 27
WEIGHT_DMAS = 12
DOWNS = 4
assert IT == DOWNS * (PAIRS // 2 - 2 - GH) + 3


def width(it):
    return min(P, INTER - it * P)


def moments(pool, stats, work, inv_counts, half_eps, minus_half, step, before):
    count = [0]

    def tt(out, a, b, op):
        ins = pool.tensor_tensor(out, a, b, op)
        count[0] += 1
        if count[0] <= 7:
            ins.then_inc(step, 1)
            pool.wait_ge(step, before + count[0])
        return ins

    tt(work[..., 2:4], stats[..., 1:3], stats[..., 4:6], ALU.add)
    tt(work[..., 0:2], work[..., 2:4], inv_counts, ALU.mult)
    tt(work[..., 4:5], stats[..., 1:2], stats[..., 4:5], ALU.subtract)
    tt(work[..., 5:6], work[..., 4:5], half_eps[..., 0:1], ALU.mult)
    tt(work[..., 4:5], work[..., 5:6], work[..., 5:6], ALU.mult)
    tt(work[..., 5:6], work[..., 4:5], work[..., 1:2], ALU.add)
    tt(work[..., 6:7], work[..., 5:6], half_eps[..., 1:2], ALU.add)
    return tt(work[..., 7:8], work[..., 6:7], minus_half, ALU.pow)


def attention(nc, x, ctx, g_xattn, wq, wk, wv, wo, bo, g, matrices, xall, stats2, ident, w_gu, d_int):
    with ExitStack() as st:
        def sb(name, shape, dt=F32):
            return st.enter_context(nc.sbuf_tensor(name, shape, dt))

        def sem(name):
            return st.enter_context(nc.semaphore(name))

        ekT = sb("ekT", [P, 2, NT, O])
        wq_sb, wk_sb, wv_sb = (ekT[:, 0, s, :].rearrange("p (t a c) -> p t a c", t=OT, a=2) for s in range(3))
        wo_sb = ekT[0:C, 0, 3, :]
        head_of_row = ekT[:, 1, 0:2, :].rearrange("r a (t o) -> r (a t) o", o=P)
        wqT_hi, wqT_lo = sb("wqT_hi", [P, O], F32R), sb("wqT_lo", [P, O], F32R)
        wkT_hi, wkT_lo = sb("wkT_hi", [P, O], F32R), sb("wkT_lo", [P, O], F32R)
        woT = sb("woT", [P, OT, C])
        foldT = sb("foldT", [P, 2, HEADS, C])
        spread = sb("spread", [P, 2 * OT, P], F32R)
        minus_spread = sb("minus_spread", [P, 2 * OT, P], F32R)
        head_sum = sb("head_sum", [P, 2, 32])
        batch_sum = sb("batch_sum", [P, 32])
        minus_half = sb("minus_half", [P, 8])
        ones = sb("ones", [P, 8])
        inv_counts, half_eps = sb("inv_counts", [P, 2]), sb("half_eps", [P, 2])
        bo_col, gate_col, g_col, tanh_col = (sb(n, [P, 1]) for n in ("bo_col", "gate_col", "g_col", "tanh_col"))

        ctx_raw = sb("ctx_raw", [P, 2, N])
        xn = sb("xn", [P, N])
        xs = sb("xs", [P, 2, 2, N], F32R)
        cs = sb("cs", [P, 2, N], F32R)
        stats = sb("stats", [P, 6])
        ln_work = sb("ln_work", [P, 8])
        qmax = sb("qmax", [P, NT, 2, HEADS])
        qmax_rows = sb("qmax_rows", [P, N], F32R)
        kneg = sb("kneg", [P, 2 * OT])
        ksum = sb("ksum", [P, 2 * OT])
        kinv = sb("kinv", [P, 2, 2 * OT])
        ek = sb("ek", [P, 2, OT, N])
        eq = sb("eq", [P, 2, 2, OT, N])
        ctxT = sb("ctxT", [P, NT, P])
        den = sb("den", [P, N])
        den_sq = sb("den_sq", [P, C])
        rden = sb("rden", [P, C])
        rden_parts = sb("rden_parts", [P, 2, C], F32R)
        rden_rows = sb("rden_rows", [P, N], F32R)
        kctxT = sb("kctxT", [P, O])
        fold = sb("fold", [P, 2 * OT, C])
        y0 = sb("y0", [P, N])
        ysq = sb("ysq", [P, N])
        ss_rows = sb("ss_rows", [32, N])
        ss_sq = sb("ss_sq", [P, 8])
        ss_max = sb("ss_max", [P, 8])
        rn_sq = sb("rn_sq", [P, 8])
        rn_parts = sb("rn_parts", [P, 2, 8], F32R)
        rn_rows = sb("rn_rows", [P, N], F32R)
        batch_of_row = sb("batch_of_row", [P, P])
        spread_batch = sb("spread_batch", [P, P], F32R)
        yn = sb("yn", [P, N])
        lane = sb("lane", [P, 1], I32)
        nibble = sb("nibble", [P, 1], I32)
        packed = sb("packed", [P, INTER], I32)
        zero = sb("zero", [P, INTER], I32)
        zero_packed = sb("zero_packed", [P, INTER // PACK], I32)

        bank = [st.enter_context(nc.psum_tensor(f"bank{i}", [P, 512], F32)) for i in range(8)]
        dve_ring = bank[0:2]
        k_ring = bank[2:4]
        act_ring = bank[4:6]
        small = bank[6:8]

        weights_in, consts_made, weights_T, wT_ready, fold_mm, fold_ready = (
            sem(n) for n in ("weights_in", "consts_made", "weights_T", "wT_ready", "fold_mm", "fold_ready"))
        gate_parts = sem("gate_parts")
        wT_hi_ready, wT_lo_ready = sem("wT_hi_ready"), sem("wT_lo_ready")
        rden_step, norm_step, ss_bounded, bn2_done, yn_ready, rn_mm = (
            sem(n) for n in ("rden_step", "norm_step", "ss_bounded", "bn2_done", "yn_ready", "rn_mm"))
        loaded = [sem("loaded_even"), sem("loaded_odd")]
        ln_stats, pool_step, rstd_ready, xn_ready = (
            sem(n) for n in ("ln_stats", "pool_step", "rstd_ready", "xn_ready"))
        x_hi, x_lo, c_hi, c_lo = (sem(n) for n in ("x_hi", "x_lo", "c_hi", "c_lo"))
        t_mm, k_mm, q_mm, kt_mm, b_mm = (sem(n) for n in ("t_mm", "k_mm", "q_mm", "kt_mm", "b_mm"))
        t_max, k_max, k_exp, kt_evac, q_exp, q_norm = (
            sem(n) for n in ("t_max", "k_max", "k_exp", "kt_evac", "q_exp", "q_norm"))
        d_mm, a_mm, m_mm, qmaxT_mm, ct_mm, f_mm, ss_mm = (
            sem(n) for n in ("d_mm", "a_mm", "m_mm", "qmaxT_mm", "ct_mm", "f_mm", "ss_mm"))
        d_evac, a_evac, m_evac, qmaxT_evac, ct_evac, y_evac, ss_evac = (
            sem(n) for n in ("d_evac", "a_evac", "m_evac", "qmaxT_evac", "ct_evac", "y_evac", "ss_evac"))
        kinv_ready, rden_ready, rn_ready, x1_done = (
            sem(n) for n in ("kinv_ready", "rden_ready", "rn_ready", "x1_done"))
        den_spread, rden_gathered, ss_spread, rn_gathered = (
            sem(n) for n in ("den_spread", "rden_gathered", "ss_spread", "rn_gathered"))

        zeros_in, packed_in = sem("zeros_in"), sem("packed_in")
        zero_ready, nib, w_int = sem("zero_ready"), sem("nib"), sem("w_int")

        def unpacked_in(p, kind):
            if kind < 2:
                return 16 * (p - 1)
            return 16 * (2 * GH + 2 * (p - 1 - 2 * GH) - (1 if isinstance(p, int) and p == PAIRS - 1 else 0))

        block = st.enter_context(nc.Block())

        x_rows = x.rearrange("(p two) c n -> p (two c) n", two=2)
        ctx_rows = ctx.rearrange("(p two) c n -> p (two c) n", two=2)

        def masks_made(eng):
            eng.wait_ge(consts_made, CONSTS_MADE)

        @block.sync
        def _(sp):
            def load(p, half, par):
                sp.dma_start(xall[:, p, :], x_rows[p]).then_inc(loaded[par], 16)
                sp.dma_start(ctx_raw[:, par, :], ctx_rows[p]).then_inc(loaded[par], 16)

            def row(ap):
                return ap.rearrange("(c one) -> c one", one=1)

            for w, dst in ((wq, wq_sb), (wk, wk_sb), (wv, wv_sb)):
                for twice in range(2):
                    sp.dma_start(dst[:, :, twice, :], w.rearrange("(t p) c -> p t c", p=P)).then_inc(weights_in, 16)
            sp.dma_start(wo_sb[:, :], wo).then_inc(weights_in, 16)
            load(0, 0, 0)
            load(1, 0, 1)
            for b in range(2):
                half = slice(b * C, (b + 1) * C)
                sp.dma_start(bo_col[half, :], row(bo)).then_inc(weights_in, 16)
                sp.dma_start(g_col[half, :], g.rearrange("one c two -> (one c) two")).then_inc(weights_in, 16)
            sp.dma_start(tanh_col[:, :], row(g_xattn).to_broadcast([P, 1])).then_inc(weights_in, 16)

            def step(p, i, par, project, combine, residual):
                if combine:
                    r = p - 1
                    sp.wait_ge(d_evac, r + 1)
                    for grp in range(4):
                        sp.dma_start(den_sq[32 * grp:32 * grp + 32, :],
                                     den[32 * grp:32 * grp + 4, :].rearrange("h (k m) -> h k m", m=C)
                                     ).then_inc(den_spread, 16)
                    sp.wait_ge(rden_ready, r + 1)
                    for part in range(2):
                        sp.dma_start(rden_rows[16 * part:16 * part + 16, :].bitcast(F32).rearrange("r (k m) -> r k m", m=C),
                                     rden_parts[:, part, :].bitcast(F32)).then_inc(rden_gathered, 16)
                if residual:
                    r2 = p - 2
                    sp.wait_ge(ss_evac, r2 + 1)
                    sp.dma_start(ss_sq[:, :],
                                 ss_rows[0:2, :].rearrange("b (k m) -> b k m", m=8)).then_inc(ss_spread, 16)
                    sp.wait_ge(rn_ready, 2 * r2 + 2)
                    for part in range(2):
                        sp.dma_start(rn_rows[2 * part:2 * part + 2, :].bitcast(F32).rearrange("b (k m) -> b k m", m=8),
                                     rn_parts[:, part, :].bitcast(F32)).then_inc(rn_gathered, 16)

            def load_weights(p, kind, k, count):
                qweight, _, zeros = matrices[kind]
                cols = qweight.shape[1]
                rows = width(k) if kind == 2 and isinstance(k, int) else P
                if not (isinstance(p, int) and p == 2):
                    sp.wait_ge(w_int, p - 2)
                sp.dma_start(zero_packed[:, 0:count * cols // PACK],
                             zeros[bass.ds(k, count), :].rearrange("g w -> (g w)").partition_broadcast(P)
                             ).then_inc(zeros_in, 16)
                for c in range(count):
                    words = qweight[bass.ds((k + c) * (GROUP // PACK), rows // PACK), :]
                    sp.dma_start(packed[0:rows, c * cols:(c + 1) * cols],
                                 words.unsqueeze(1).to_broadcast([rows // PACK, PACK, cols])).then_inc(packed_in, 16)

            def step_and_load(p, i, par, project, combine, residual, weights=None):
                if weights:
                    load_weights(p, *weights)
                step(p, i, par, project, combine, residual)
                sp.wait_ge(ct_mm, p + 1)
                load(p + 2, i + 1, par)

            step_and_load(0, 0, 0, True, False, False)
            step_and_load(1, 0, 1, True, True, False)
            with sp.Fori(1, GH + 1) as i:
                step_and_load(2 * i, i, 0, True, True, True, (0, i - 1, 1))
                step_and_load(2 * i + 1, i, 1, True, True, True, (1, i - 1, 1))
            with sp.Fori(GH + 1, PAIRS // 2 - 1) as i:
                step_and_load(2 * i, i, 0, True, True, True, (2, DOWNS * i - DOWNS * (GH + 1), 2))
                step_and_load(2 * i + 1, i, 1, True, True, True, (2, DOWNS * i - DOWNS * (GH + 1) + 2, 2))
            load_weights(PAIRS - 2, 2, IT - 3, 2)
            step(PAIRS - 2, 0, 0, True, True, True)
            load_weights(PAIRS - 1, 2, IT - 1, 1)
            step(PAIRS - 1, 0, 1, True, True, True)
            step(PAIRS, 0, 0, False, True, True)
            step(PAIRS + 1, 0, 1, False, False, True)

        @block.gpsimd
        def _(pool):
            made = [0]

            def then(ins):
                made[0] += 1
                ins.then_inc(consts_made, 1)
                pool.wait_ge(consts_made, made[0])

            then(pool.iota(lane[:, :], [[0, 1]], base=0, channel_multiplier=4))
            then(pool.memset(ident[:, :], 0.0))
            then(pool.memset(head_of_row[:, :, :], 0.0))
            then(pool.memset(head_sum[:, :, :], 0.0))
            then(pool.memset(foldT[:, :, :, :], 0.0))
            then(pool.memset(batch_sum[:, :], 0.0))
            then(pool.memset(minus_half[:, :], -0.5))
            then(pool.memset(ones[:, :], 1.0))
            then(pool.memset(inv_counts[:, 0:1], 0.5))
            then(pool.memset(inv_counts[:, 1:2], 1.0 / N))
            then(pool.memset(half_eps[:, 0:1], 0.5))
            then(pool.memset(half_eps[:, 1:2], EPS))
            then(pool.memset(qmax_rows[:, :].bitcast(F32), 0.0))
            then(pool.memset(rden_rows[:, :].bitcast(F32), 0.0))
            then(pool.memset(rn_rows[:, :].bitcast(F32), 0.0))
            then(pool.memset(batch_of_row[:, :], 0.0))
            then(pool.affine_select(out=ident[:, :], in_=ident[:, :], compare_op=ALU.not_equal, fill=1.0, base=0,
                                    pattern=[[-1, P]], channel_multiplier=1))
            rows = head_of_row[:, :, :].rearrange("r bt (e d) -> r bt e d", e=2)
            for part in range(2):
                then(pool.affine_select(out=rows, in_=rows, compare_op=ALU.not_equal, fill=1.0, base=-16 * part,
                                        pattern=[[-2, 2 * OT], [-1, 2], [0, DH]], channel_multiplier=1))
            rows = batch_of_row[:, :].rearrange("r (b c) -> r b c", b=2)
            for part in range(2):
                then(pool.affine_select(out=rows, in_=rows, compare_op=ALU.not_equal, fill=1.0, base=-2 * part,
                                        pattern=[[-1, 2], [0, C]], channel_multiplier=1))
            for e in range(2):
                half = slice(e * DH, (e + 1) * DH)
                for tt in range(2):
                    then(pool.memset(head_sum[half, tt, :].rearrange("o (m f) -> o m f", f=4)[:, :, 2 * tt + e],
                                     float(DH) ** 0.5))
                then(pool.memset(batch_sum[half, :].rearrange("o (m f) -> o m f", f=2)[:, :, e], 1.0))
            assert made[0] == CONSTS_MADE

            def layernorm(p):
                pool.wait_ge(ln_stats, p + 1)
                moments(pool, stats[:, :], ln_work[:, :], inv_counts[:, :], half_eps[:, :], minus_half[:, 0:1], pool_step,
                        7 * p).then_inc(rstd_ready, 1)
                pool.wait_ge(rstd_ready, p + 1)

            def inverse_norm(r):
                pool.wait_ge(ss_bounded, r + 1)
                pool.tensor_tensor(rn_sq[:, :], ss_max[:, :], minus_half[:, :], ALU.pow).then_inc(norm_step, 1)
                pool.wait_ge(norm_step, r + 1)
                pool.tensor_tensor(rn_parts[:, 0, :], rn_sq[:, :], ones[:, :], ALU.mult).then_inc(rn_ready, 1)
                pool.wait_ge(rn_ready, 2 * r + 1)
                pool.tensor_tensor(rn_parts[:, 1, :], rn_sq[:, :], rn_parts[:, 0, :].bitcast(F32),
                                   ALU.subtract).then_inc(rn_ready, 1)
                pool.wait_ge(rn_ready, 2 * r + 2)

            def low_parts(p, hi_ready, raw, split, lo_ready):
                for b in range(2):
                    rows, other = slice(b * C, (b + 1) * C), slice((1 - b) * C, (2 - b) * C)
                    pool.wait_ge(hi_ready, 2 * p + b + 1)
                    pool.tensor_tensor(split[other, b, :], raw[rows], split[rows, b, :].bitcast(F32),
                                       ALU.subtract).then_inc(lo_ready, 1)
                    pool.wait_ge(lo_ready, 2 * p + b + 1)

            def step(p, par, residual, following=True):
                if following:
                    layernorm(p + 1)
                    low_parts(p + 1, c_hi, ctx_raw[:, 1 - par, :], cs, c_lo)
                if residual:
                    inverse_norm(p - 2)
                if following:
                    low_parts(p + 1, x_hi, xn[:, :], xs[:, 1 - par], x_lo)

            pool.wait_ge(consts_made, made[0])
            layernorm(0)
            low_parts(0, c_hi, ctx_raw[:, 0, :], cs, c_lo)
            low_parts(0, x_hi, xn[:, :], xs[:, 0], x_lo)
            step(0, 0, False)
            step(1, 1, False)
            with pool.Fori(1, PAIRS // 2 - 1) as i:
                step(2 * i, 0, True)
                step(2 * i + 1, 1, True)
            step(PAIRS - 2, 0, True)
            for p in range(PAIRS - 1, PAIRS + 2):
                step(p, p % 2, True, False)

        def k_slot(b, t):
            return b * OT + t

        @block.scalar
        def _(act):
            act.wait_ge(weights_T, 1)
            act.activation(wqT_hi[:, :], bank[0][:, :], ACT.Copy).then_inc(wT_hi_ready, 1)
            act.wait_ge(weights_T, 2)
            act.activation(wkT_hi[:, :], bank[1][:, :], ACT.Copy, scale=-1.0).then_inc(wT_hi_ready, 1)
            act.wait_ge(weights_T, 3)
            act.activation(woT[:, :, :].rearrange("p t c -> p (t c)"), bank[2][:, 0:OT * C], ACT.Copy).then_inc(wT_ready, 1)
            act.wait_ge(consts_made, CONSTS_MADE)
            act.activation(spread[:, :, :], head_of_row[:, :, :], ACT.Copy).then_inc(wT_ready, 1)
            act.activation(spread_batch[:, :], batch_of_row[:, :], ACT.Copy).then_inc(wT_ready, 1)
            act.activation(minus_spread[:, :, :], head_of_row[:, :, :], ACT.Copy, scale=-1.0).then_inc(wT_ready, 1)
            act.wait_ge(fold_mm, 1)
            for b in range(2):
                rows = slice(b * C, (b + 1) * C)
                for e in range(2):
                    act.activation(foldT[rows, b, e::2, :], bank[3 + e][rows, :].rearrange("c (h d) -> c h d", d=C)[:, e::2, :],
                                   ACT.Copy).then_inc(fold_ready, 1)
            act.wait_ge(weights_in, 16 * WEIGHT_DMAS)
            act.activation(tanh_col[:, :], tanh_col[:, :], ACT.Tanh).then_inc(gate_parts, 1)

            def ctx_high(p, half, par):
                act.wait_ge(loaded[par], 32 * (half + 1))
                for b in range(2):
                    rows = slice(b * C, (b + 1) * C)
                    act.activation(cs[rows, b, :], ctx_raw[rows, par, :], ACT.Copy).then_inc(c_hi, 1)

            def x_high(p, par):
                act.wait_ge(xn_ready, p + 1)
                for b in range(2):
                    rows = slice(b * C, (b + 1) * C)
                    act.activation(xs[rows, par, b, :], xn[rows, :], ACT.Copy).then_inc(x_hi, 1)

            ctx_high(0, 0, 0)
            x_high(0, 0)

            def step(p, i, par, project, combine, residual, last=False):
                r = p - 1
                first = isinstance(p, int) and p == 0

                def k_exp_tile(b, t):
                    n = 8 * p + b * OT + t
                    act.wait_ge(k_max, n + 1)
                    if t == 0 and not first:
                        act.wait_ge(kt_mm, 8 * p - 4 + 4 * b)
                        if b == 0:
                            act.wait_ge(kinv_ready, p)
                    act.activation(ek[:, b, t, :], k_ring[t % 2][:, :], ACT.Exp, bias=kneg[:, k_slot(b, t):k_slot(b, t) + 1],
                                   scale=-1.0, accum_out=ksum[:, k_slot(b, t):k_slot(b, t) + 1]).then_inc(k_exp, 1)

                def k_transposed(b, t):
                    act.wait_ge(kt_mm, 8 * p + 4 * b + t + 1)
                    act.activation(ekT[:, b, t, :], act_ring[t % 2][:, :], ACT.Copy).then_inc(kt_evac, 1)

                def q_exp_tile(b, t):
                    act.wait_ge(q_mm, 8 * p + 4 * b + t + 1)
                    act.activation(eq[:, par, b, t, :], act_ring[t % 2][:, :], ACT.Exp).then_inc(q_exp, 1)

                if project:
                    k_exp_tile(0, 0)
                if combine:
                    act.wait_ge(d_mm, r + 1)
                    act.activation(den[:, :], small[0][:, :], ACT.Copy).then_inc(d_evac, 1)
                if project:
                    for t in range(1, OT):
                        k_exp_tile(0, t)
                    k_exp_tile(1, 0)
                    k_exp_tile(1, 1)
                if combine:
                    act.wait_ge(a_mm, r + 1)
                    act.activation(kctxT[:, :], small[1][:, :], ACT.Copy).then_inc(a_evac, 1)
                if project:
                    k_exp_tile(1, 2)
                    k_exp_tile(1, 3)
                    for t in range(3):
                        k_transposed(0, t)
                    act.wait_ge(qmaxT_mm, p + 1)
                    act.activation(qmax_rows[0:16, :], small[0][0:16, :], ACT.Copy).then_inc(qmaxT_evac, 1)
                if residual:
                    act.wait_ge(f_mm, r)
                    act.activation(y0[:, :], small[1][:, :], ACT.Identity, bias=bo_col[:, 0:1]).then_inc(y_evac, 1)
                    act.activation(ysq[:, :], small[1][:, :], ACT.Square, bias=bo_col[:, 0:1]).then_inc(y_evac, 1)
                if project:
                    k_transposed(0, 3)
                    if not last:
                        act.wait_ge(k_mm, 8 * p + 8)
                        ctx_high(p + 1, i + par, 1 - par)
                    q_exp_tile(0, 0)
                    q_exp_tile(0, 1)
                if residual:
                    act.wait_ge(ss_mm, r)
                    act.activation(ss_rows[:, :], small[0][0:32, :], ACT.Copy).then_inc(ss_evac, 1)
                if project:
                    q_exp_tile(0, 2)
                    q_exp_tile(0, 3)
                    for t in range(NT):
                        k_transposed(1, t)
                    if not last:
                        x_high(p + 1, 1 - par)
                    for t in range(OT):
                        q_exp_tile(1, t)
                    act.wait_ge(ct_mm, p + 1)
                    act.activation(ctxT[:, :, :].rearrange("n t c -> n (t c)"), small[0][:, :], ACT.Copy).then_inc(ct_evac, 1)
                if residual:
                    act.wait_ge(yn_ready, r)

            step(0, 0, 0, True, False, False)
            step(1, 0, 1, True, True, False)
            with act.Fori(1, PAIRS // 2 - 1) as i:
                step(2 * i, i, 0, True, True, True)
                step(2 * i + 1, i, 1, True, True, True)
            step(PAIRS - 2, PAIRS // 2 - 1, 0, True, True, True)
            step(PAIRS - 1, PAIRS // 2 - 1, 1, True, True, True, last=True)
            step(PAIRS, PAIRS // 2, 0, False, True, True)
            step(PAIRS + 1, PAIRS // 2, 1, False, False, True)

        @block.tensor
        def _(pe):
            pe.wait_ge(consts_made, CONSTS_MADE)
            pe.wait_ge(weights_in, 16 * WEIGHT_DMAS)
            for w, ps in ((wq_sb, bank[0]), (wk_sb, bank[1])):
                for t in range(OT):
                    last = pe.transpose(ps[:, t * P:(t + 1) * P], w[:, t, :, :].rearrange("p a c -> p (a c)"), ident[:, :])
                last.then_inc(weights_T, 1)
            for t in range(OT):
                last = pe.transpose(bank[2][:, t * C:(t + 1) * C], wo_sb[:, t * P:(t + 1) * P], ident[0:C, 0:C])
            last.then_inc(weights_T, 1)
            pe.wait_ge(wT_ready, 1)
            for h in range(HEADS):
                rows = slice((h % 2) * DH, (h % 2 + 1) * DH)
                last = pe.matmul(bank[3 + h % 2][:, h * C:(h + 1) * C], wv_sb[rows, h // 2, :, :].rearrange("p a c -> p (a c)"),
                                 woT[rows, h // 2, :], start=True, stop=True)
            last.then_inc(fold_mm, 1)
            pe.wait_ge(wT_ready, 4)
            pe.wait_ge(wT_lo_ready, 2)
            pe.wait_ge(fold_ready, 4)

            def step(p, i, par, project, combine, residual):
                r = p - 1
                first = isinstance(p, int) and p == 0
                qpar = 1 - par

                def t_and_k(b, t):
                    if not project:
                        return
                    n = 8 * p + 4 * b + t
                    if b == 0 and t < 2:
                        if residual:
                            pe.wait_ge(q_norm, 8 * r - 1 + t)
                    else:
                        pe.wait_ge(t_max, n - 1)
                    if t == 0:
                        pe.wait_ge(x_lo, 2 * p + b + 1)
                    pe.matmul(dve_ring[t % 2][:, :], xs[:, par, b, t * P:(t + 1) * P], wqT_hi[:, :],
                              start=True, stop=True).then_inc(t_mm, 1)
                    if not (first and b == 0 and t < 2):
                        pe.wait_ge(k_exp, n - 1)
                    if t == 0:
                        pe.wait_ge(c_lo, 2 * p + b + 1)
                    pe.matmul(k_ring[t % 2][:, :], wkT_hi[:, t * P:(t + 1) * P], cs[:, b, :], start=True, stop=False)
                    pe.matmul(k_ring[t % 2][:, :], wkT_lo[:, t * P:(t + 1) * P], cs[:, b, :],
                              start=False, stop=True).then_inc(k_mm, 1)

                def denominators(tt):
                    if not combine:
                        return
                    if tt == 0:
                        pe.wait_ge(q_exp, 8 * r + 8)
                        pe.wait_ge(ct_evac, r + 1)
                    for grp in range(4):
                        b, t = grp // 2, 2 * (grp % 2) + tt
                        last = pe.matmul(small[0][32 * grp:32 * grp + 32, :], head_sum[:, tt, :], eq[:, qpar, b, t, :],
                                         start=(tt == 0), stop=(tt == 1))
                    if tt == 1:
                        last.then_inc(d_mm, 1)

                def context(t):
                    if not combine:
                        return
                    if t == 0:
                        pe.wait_ge(kt_evac, 8 * r + 8)
                        pe.wait_ge(ct_evac, r + 1)
                        if residual:
                            pe.wait_ge(m_evac, r)
                    for b in range(2):
                        last = pe.matmul(small[1][b * C:(b + 1) * C, :], ctxT[:, t, b * C:(b + 1) * C], ekT[:, b, t, :],
                                         start=(t == 0), stop=(t == NT - 1))
                    if t == NT - 1:
                        last.then_inc(a_mm, 1)

                def q_max_rows():
                    if not project:
                        return
                    pe.wait_ge(t_max, 8 * p + 8)
                    if combine:
                        pe.wait_ge(d_evac, r + 1)
                    for t in range(NT):
                        last = pe.transpose(small[0][0:16, t * P:(t + 1) * P],
                                            qmax[:, t, :, :].rearrange("n b h -> n (b h)"), ident[:, :])
                    last.then_inc(qmaxT_mm, 1)

                def act_ring_free(kind, b, t):
                    if t >= 2:
                        pe.wait_ge(kt_evac if kind == "kt" else q_exp, 8 * p + 4 * b + t - 1)
                    elif kind == "q":
                        pe.wait_ge(kt_evac, 8 * p + 4 * b + t + 3)
                    elif b == 1:
                        pe.wait_ge(q_exp, 8 * p + t + 3)
                    elif not first:
                        pe.wait_ge(q_exp, 8 * p - 1 + t)

                def k_transposed(b, t):
                    if not project:
                        return
                    act_ring_free("kt", b, t)
                    if t == 0:
                        pe.wait_ge(k_exp, 8 * p + 4 * b + 4)
                    for ot in range(OT):
                        last = pe.transpose(act_ring[t % 2][:, ot * P:(ot + 1) * P], ek[:, b, ot, t * P:(t + 1) * P], ident[:, :])
                    last.then_inc(kt_mm, 1)

                def q_logits(b, t):
                    if not project:
                        return
                    act_ring_free("q", b, t)
                    if b == 0 and t == 0:
                        pe.wait_ge(qmaxT_evac, p + 1)
                    out, cols = act_ring[t % 2][:, :], slice(t * P, (t + 1) * P)
                    pe.matmul(out, wqT_hi[:, cols], xs[:, par, b, :], start=True, stop=False)
                    pe.matmul(out, wqT_lo[:, cols], xs[:, par, b, :], start=False, stop=False)
                    pe.matmul(out, minus_spread[:, k_slot(b, t), :], qmax_rows[:, :], start=False,
                              stop=True).then_inc(q_mm, 1)

                def fold_context():
                    if not combine:
                        return
                    pe.wait_ge(a_evac, r + 1)
                    if residual:
                        pe.wait_ge(y_evac, 2 * r)
                    for b in range(2):
                        for t in range(OT):
                            for e in range(2):
                                last = pe.matmul(small[1][e * DH:(e + 1) * DH, k_slot(b, t) * C:(k_slot(b, t) + 1) * C],
                                                 kctxT[:, t * P + e * DH:t * P + (e + 1) * DH],
                                                 foldT[:, b, 2 * t + e, :], start=True, stop=True)
                    last.then_inc(m_mm, 1)

                def spread_reciprocals(b, t):
                    if not combine:
                        return
                    n = 8 * r + 4 * b + t
                    if b == 0 and t == 0:
                        pe.wait_ge(rden_gathered, 32 * (r + 1))
                    if b == 0 and t < 2 and project:
                        pe.wait_ge(t_max, 8 * p + 8)
                    else:
                        pe.wait_ge(q_norm, n - 1)
                    pe.matmul(dve_ring[t % 2][:, :], spread[:, k_slot(b, t), :], rden_rows[:, :],
                              start=True, stop=True).then_inc(b_mm, 1)

                def ctx_transposed():
                    if not project:
                        return
                    pe.wait_ge(loaded[par], 32 * (i + 1))
                    pe.wait_ge(qmaxT_evac, p + 1)
                    if residual:
                        pe.wait_ge(ss_evac, r)
                    for t in range(NT):
                        last = pe.transpose(small[0][:, t * P:(t + 1) * P], ctx_raw[:, par, t * P:(t + 1) * P], ident[:, :])
                    last.then_inc(ct_mm, 1)

                def spread_inverse_norm():
                    if not residual:
                        return
                    pe.wait_ge(rn_gathered, 32 * (r - 1) + 32)
                    if combine:
                        pe.wait_ge(m_evac, r + 1)
                    else:
                        pe.wait_ge(y_evac, 2 * r)
                    pe.matmul(small[1][:, :], spread_batch[:, :], rn_rows[:, :], start=True, stop=True).then_inc(rn_mm, 1)

                def output(t):
                    if not residual:
                        return
                    if t == 0:
                        pe.wait_ge(q_norm, 8 * r)
                        pe.wait_ge(m_evac, r)
                        if combine:
                            pe.wait_ge(a_evac, r + 1)
                    for b in range(2):
                        last = pe.matmul(small[1][b * C:(b + 1) * C, :], fold[:, k_slot(b, t), :], eq[:, par, b, t, :],
                                         start=(t == 0), stop=(t == OT - 1))
                    if t == OT - 1:
                        last.then_inc(f_mm, 1)

                def squared_norms():
                    if not residual:
                        return
                    pe.wait_ge(y_evac, 2 * r)
                    if project:
                        pe.wait_ge(qmaxT_evac, p + 1)
                    elif combine:
                        pe.wait_ge(d_evac, r + 1)
                    else:
                        pe.wait_ge(ss_evac, r - 1)
                    pe.matmul(small[0][0:32, :], batch_sum[:, :], ysq[:, :], start=True, stop=True).then_inc(ss_mm, 1)

                t_and_k(0, 0)
                denominators(0)
                denominators(1)
                t_and_k(0, 1)
                context(0)
                t_and_k(0, 2)
                t_and_k(0, 3)
                context(1)
                t_and_k(1, 0)
                context(2)
                t_and_k(1, 1)
                context(3)
                t_and_k(1, 2)
                t_and_k(1, 3)
                output(0)
                k_transposed(0, 0)
                output(1)
                k_transposed(0, 1)
                output(2)
                k_transposed(0, 2)
                q_max_rows()
                output(3)
                k_transposed(0, 3)
                q_logits(0, 0)
                q_logits(0, 1)
                squared_norms()
                fold_context()
                spread_reciprocals(0, 0)
                q_logits(0, 2)
                spread_reciprocals(0, 1)
                q_logits(0, 3)
                spread_reciprocals(0, 2)
                k_transposed(1, 0)
                spread_reciprocals(0, 3)
                k_transposed(1, 1)
                spread_reciprocals(1, 0)
                k_transposed(1, 2)
                spread_reciprocals(1, 1)
                k_transposed(1, 3)
                spread_reciprocals(1, 2)
                q_logits(1, 0)
                spread_reciprocals(1, 3)
                q_logits(1, 1)
                spread_inverse_norm()
                q_logits(1, 2)
                q_logits(1, 3)
                ctx_transposed()
                if residual:
                    pe.wait_ge(yn_ready, r)

            step(0, 0, 0, True, False, False)
            step(1, 0, 1, True, True, False)
            with pe.Fori(1, PAIRS // 2) as i:
                step(2 * i, i, 0, True, True, True)
                step(2 * i + 1, i, 1, True, True, True)
            step(PAIRS, PAIRS // 2, 0, False, True, True)
            step(PAIRS + 1, PAIRS // 2, 1, False, False, True)

        @block.vector
        def _(dve):
            for n, (ps, hi, lo, sign) in enumerate(((bank[0], wqT_hi, wqT_lo, 1.0), (bank[1], wkT_hi, wkT_lo, -1.0))):
                dve.wait_ge(wT_hi_ready, n + 1)
                dve.scalar_tensor_tensor(out=lo[:, :], in0=ps[:, :], scalar=sign, in1=hi[:, :].bitcast(F32), op0=ALU.mult,
                                         op1=ALU.subtract).then_inc(wT_lo_ready, 1)
            dve.wait_ge(gate_parts, 1)
            dve.tensor_scalar(gate_col[:, :], g_col[:, :], tanh_col[:, 0:1], float(C) ** 0.5, ALU.mult,
                              ALU.mult).then_inc(gate_parts, 1)

            dve.wait_ge(gate_parts, 2)
            dve.wait_ge(consts_made, CONSTS_MADE)
            dve.tensor_scalar(nibble[:, :], lane[:, :], 31, None, ALU.bitwise_and).then_inc(nib, 1)

            def unpack(p, kind, k, count):
                cols = count * matrices[kind][0].shape[1]
                rows = width(k) if kind == 2 and isinstance(k, int) else P
                dve.wait_ge(zeros_in, 16 * (p - 1))
                if not (isinstance(p, int) and p == 2):
                    dve.wait_ge(w_int, p - 2)
                for e in range(PACK):
                    last = dve.tensor_scalar(zero[:, 0:cols].rearrange("p (w e) -> p w e", e=PACK)[:, :, e],
                                             zero_packed[:, 0:cols // PACK], 4 * e, 15,
                                             ALU.logical_shift_right, ALU.bitwise_and)
                last.then_inc(zero_ready, 1)
                word, z = packed[0:rows, 0:cols], zero[0:rows, 0:cols]
                dve.wait_ge(packed_in, unpacked_in(p, kind))
                dve.tensor_scalar(word, word, nibble[0:rows, 0:1], 15, ALU.logical_shift_right,
                                  ALU.bitwise_and).then_inc(nib, 1)
                dve.wait_ge(nib, p)
                dve.wait_ge(zero_ready, p - 1)
                if kind == 2:
                    out = d_int[0:rows, bass.ds(k, count), :]
                    word, z = (a.rearrange("p (g n) -> p g n", g=count) for a in (word, z))
                else:
                    out = w_gu[:, kind, bass.ds(k, 1), :]
                    word, z = word.unsqueeze(1), z.unsqueeze(1)
                dve.scalar_tensor_tensor(out=out, in0=word, scalar=1.0, in1=z, op0=ALU.subtract,
                                         op1=ALU.subtract).then_inc(w_int, 1)

            def layernorm_stats(p, half, par):
                masks_made(dve)
                dve.wait_ge(loaded[par], 32 * (half + 1))
                if not (isinstance(p, int) and p == 0):
                    dve.wait_ge(rstd_ready, p)
                dve.bn_stats(stats[:, :], xall[:, p, :]).then_inc(ln_stats, 1)

            def layernorm_apply(p):
                dve.wait_ge(rstd_ready, p + 1)
                if not (isinstance(p, int) and p == 0):
                    dve.wait_ge(x_lo, 2 * p)
                dve.tensor_scalar(xn[:, :], xall[:, p, :], ln_work[:, 0:1], ln_work[:, 7:8], ALU.subtract,
                                  ALU.mult).then_inc(xn_ready, 1)

            layernorm_stats(0, 0, 0)
            layernorm_apply(0)

            def step(p, i, par, project, combine, residual, last=False, weights=None):
                r, r2 = p - 1, p - 2

                def maxima(b, t):
                    n = 8 * p + 4 * b + t
                    dve.wait_ge(t_mm, n + 1)
                    dve.tensor_reduce(qmax[:, t, b, :], dve_ring[t % 2][:, :].rearrange("n (h d) -> n h d", d=DH),
                                      AX.X, ALU.max).then_inc(t_max, 1)
                    dve.wait_ge(k_mm, n + 1)
                    dve.tensor_reduce(kneg[:, k_slot(b, t):k_slot(b, t) + 1], k_ring[t % 2][:, :], AX.X,
                                      ALU.min).then_inc(k_max, 1)

                def normalise(b, t):
                    n = 8 * r + 4 * b + t
                    dve.wait_ge(b_mm, n + 1)
                    e = eq[:, 1 - par, b, t, :]
                    dve.tensor_tensor(e, e, dve_ring[t % 2][:, :], ALU.mult).then_inc(q_norm, 1)

                if project:
                    for t in range(4):
                        maxima(0, t)
                    if not last:
                        layernorm_stats(p + 1, i + par, 1 - par)
                    for t in range(4):
                        maxima(1, t)
                if combine:
                    dve.wait_ge(den_spread, 64 * (r + 1))
                    dve.reciprocal(rden[:, :], den_sq[:, :]).then_inc(rden_step, 1)
                    dve.wait_ge(rden_step, 2 * r + 1)
                    if residual:
                        dve.wait_ge(rden_gathered, 32 * r)
                    dve.tensor_copy(rden_parts[:, 0, :], rden[:, :]).then_inc(rden_step, 1)
                    dve.wait_ge(rden_step, 2 * r + 2)
                    dve.tensor_tensor(rden_parts[:, 1, :], rden[:, :], rden_parts[:, 0, :].bitcast(F32),
                                      ALU.subtract).then_inc(rden_ready, 1)
                if project and not last:
                    layernorm_apply(p + 1)
                if weights:
                    unpack(p, *weights)
                if combine:
                    normalise(0, 0)
                    normalise(0, 1)
                if residual:
                    dve.wait_ge(ss_spread, 16 * (r2 + 1))
                    dve.tensor_scalar(ss_max[:, :], ss_sq[:, :], 1e-24, None, ALU.max).then_inc(ss_bounded, 1)
                if combine:
                    normalise(0, 2)
                    dve.wait_ge(m_mm, r + 1)
                    dve.wait_ge(kinv_ready, r + 1)
                    dve.tensor_tensor(fold[:, :, :], small[1][:, :].rearrange("o (s c) -> o s c", c=C),
                                      kinv[:, 1 - par, :].unsqueeze(2).to_broadcast([P, 2 * OT, C]),
                                      ALU.mult).then_inc(m_evac, 1)
                    normalise(0, 3)
                    for t in range(OT):
                        normalise(1, t)
                if residual:
                    dve.wait_ge(rn_mm, r2 + 1)
                    dve.wait_ge(y_evac, 2 * (r2 + 1))
                    dve.tensor_tensor(yn[:, :], y0[:, :], small[1][:, :], ALU.mult).then_inc(yn_ready, 1)
                    dve.wait_ge(yn_ready, r2 + 1)
                    dve.scalar_tensor_tensor(out=xall[:, r2, :], in0=yn[:, :], scalar=gate_col[:, 0:1],
                                             in1=xall[:, r2, :], op0=ALU.mult, op1=ALU.add).then_inc(x1_done, 1)
                if project:
                    dve.wait_ge(k_exp, 8 * p + 8)
                    dve.reciprocal(kinv[:, par, :], ksum[:, :]).then_inc(kinv_ready, 1)
                if residual:
                    masks_made(dve)
                    dve.wait_ge(x1_done, r2 + 1)
                    dve.bn_stats(stats2[:, r2, :], xall[:, r2, :]).then_inc(bn2_done, 1)

            step(0, 0, 0, True, False, False)
            step(1, 0, 1, True, True, False)
            with dve.Fori(1, GH + 1) as i:
                step(2 * i, i, 0, True, True, True, weights=(0, i - 1, 1))
                step(2 * i + 1, i, 1, True, True, True, weights=(1, i - 1, 1))
            with dve.Fori(GH + 1, PAIRS // 2 - 1) as i:
                step(2 * i, i, 0, True, True, True, weights=(2, DOWNS * i - DOWNS * (GH + 1), 2))
                step(2 * i + 1, i, 1, True, True, True, weights=(2, DOWNS * i - DOWNS * (GH + 1) + 2, 2))
            step(PAIRS - 2, PAIRS // 2 - 1, 0, True, True, True, weights=(2, IT - 3, 2))
            step(PAIRS - 1, PAIRS // 2 - 1, 1, True, True, True, last=True, weights=(2, IT - 1, 1))
            step(PAIRS, PAIRS // 2, 0, False, True, True)
            step(PAIRS + 1, PAIRS // 2, 1, False, False, True)
            dve.wait_ge(bn2_done, PAIRS)
            dve.wait_ge(w_int, PAIRS - 2)


def feed_forward(nc, xall, stats2, ident, w_gu, d_int, g_ffn, gate_scales, up_scales, down_scales, out):
    with ExitStack() as st:
        def sb(name, shape, dt=F32):
            return st.enter_context(nc.sbuf_tensor(name, shape, dt))

        def sem(name):
            return st.enter_context(nc.semaphore(name))

        minus_half = sb("minus_half2", [P, PAIRS])
        wd_hi, wd_lo = sb("wd_hi", [P, IT, N], F32R), sb("wd_lo", [P, IT, N], F32R)
        d_scale = sb("d_scale", [P, IT, N], F16)
        s_rows16 = sb("s_rows16", [2 * GH, INTER], F16)
        scale_T = sb("scale_T", [P, IT, 2 * GH])
        ln_work = sb("ln_work2", [P, PAIRS, 8])
        rstd = sb("rstd2", [P, PAIRS])
        inv_counts, half_eps = sb("inv_counts2", [P, PAIRS, 2]), sb("half_eps2", [P, PAIRS, 2])
        xn = sb("xn2", [P, 2, N])
        xT_hi, xT_lo = sb("xT_hi", [P, GH, ROWS], F16), sb("xT_lo", [P, GH, ROWS], F16)
        tanh_col = sb("tanh_col2", [P, 1])
        acc = sb("acc", [P, 3, 2, CHUNK])
        s_rows = acc[0:2 * GH, :, :, :].rearrange("p a b c -> p (a b c)")[:, 0:INTER]
        sig = sb("sig", [P, CHUNK])
        act_gate = sb("act_gate", [P, CHUNK])
        inter = sb("inter", [P, CHUNK])
        in_hi, in_lo = sb("in_hi", [P, 3, CHUNK], F32R), sb("in_lo", [P, 3, CHUNK], F32R)
        y16 = sb("y16", [P, TPC, N], F16)

        bank = [st.enter_context(nc.psum_tensor(f"ffn_bank{i}", [P, 512], F32)) for i in range(8)]
        y_bank = bank[0:4]
        gu_bank = bank[4:8]

        small_in, made, d_scale_in = sem("small_in"), sem("made"), sem("d_scale_in")
        s_cast, sT_mm, sT_ready, tanh_ready = sem("s_cast"), sem("sT_mm"), sem("sT_ready"), sem("tanh_ready")
        d_scaled, d_hi, d_lo = (sem(n) for n in ("d_scaled", "d_hi", "d_lo"))
        rstd_step, xn_ready, xT_mm, xT_hi_ready, xT_lo_ready = (
            sem(n) for n in ("rstd_step", "xn2_ready", "xT_mm", "xT_hi_ready", "xT_lo_ready"))
        gu_mm, s0_done, acc_done, sig_ready, gs_ready, inter_ready, in_hi_ready, in_lo_ready, down_mm = (
            sem(n) for n in ("gu_mm", "s0_done", "acc_done", "sig_ready", "gs_ready", "inter_ready", "in_hi_ready",
                             "in_lo_ready", "down_mm"))
        y16_ready, out_ready, stored = sem("y16_ready"), sem("out_ready"), sem("stored")

        block = st.enter_context(nc.Block())

        def last_unit(j, it, first):
            if it:
                return j, it - 1, first
            return None if first else (j - 1, IT - 1, isinstance(j, int) and j == 1)

        def two_units_back(j, it, first):
            return last_unit(*last_unit(j, it, first))

        def projected(j, it, first=None):
            return (IT - 1 + TPC) * j + (it + 1 if it < IT - 1 else it + TPC)

        @block.sync
        def _(sp):
            sp.dma_start(s_rows16[0:GH, :], gate_scales).then_inc(small_in, 16)
            sp.dma_start(s_rows16[GH:2 * GH, :], up_scales).then_inc(small_in, 16)
            sp.dma_start(tanh_col[:, :], g_ffn.rearrange("(c one) -> c one", one=1).to_broadcast([P, 1])).then_inc(small_in, 16)
            sp.dma_start(d_scale[:, :, :].rearrange("p g n -> p (g n)"),
                         down_scales.rearrange("g n -> (g n)").partition_broadcast(P)).then_inc(d_scale_in, 16)
            out_rows = out.rearrange("(p two) c n -> p (two c) n", two=2)
            with sp.Fori(0, PAIRS) as tile:
                sp.wait_ge(out_ready, tile + 1)
                sp.dma_start(out_rows[tile], xall[:, tile, :]).then_inc(stored, 16)
            sp.wait_ge(stored, 16 * PAIRS)

        @block.gpsimd
        def _(pool):
            pool.memset(minus_half[:, :], -0.5).then_inc(made, 1)
            for col, (t, value) in enumerate(((inv_counts, 0.5), (inv_counts, 1.0 / N), (half_eps, 0.5), (half_eps, EPS))):
                pool.memset(t[:, :, col % 2], value).then_inc(made, 1)
            pool.wait_ge(made, 5)
            moments(pool, stats2[:, :, :], ln_work[:, :, :], inv_counts[:, :, :], half_eps[:, :, :], minus_half[:, :].unsqueeze(2), rstd_step,
                    0).then_inc(rstd_step, 1)
            pool.wait_ge(rstd_step, 8)
            pool.tensor_scalar(rstd[:, :], ln_work[:, :, 7], XSCALE, None, ALU.mult).then_inc(rstd_step, 1)

            def low_part(j, it, first):
                n, w = IT * j + it, width(it)
                pool.wait_ge(in_hi_ready, n + 1)
                if not (first and it < 2):
                    pool.wait_ge(down_mm, projected(*two_units_back(j, it, first)))
                pool.tensor_tensor(in_lo[0:w, it % 3, :], inter[0:w, :], in_hi[0:w, it % 3, :].bitcast(F32),
                                   ALU.subtract).then_inc(in_lo_ready, 1)

            for it in range(IT):
                low_part(0, it, True)
            with pool.Fori(1, CHUNKS) as j:
                for it in range(IT):
                    low_part(j, it, False)

        @block.scalar
        def _(act):
            act.wait_ge(small_in, 48)
            act.activation(tanh_col[:, :], tanh_col[:, :], ACT.Tanh).then_inc(tanh_ready, 1)
            act.activation(s_rows, s_rows16[:, :], ACT.Copy, scale=1.0 / XSCALE).then_inc(s_cast, 1)
            act.wait_ge(sT_mm, 1)
            act.activation(scale_T[:, 0:IT - 1, :].rearrange("p i s -> p (i s)"), bank[4][:, 0:(IT - 1) * 8], ACT.Copy).then_inc(sT_ready, 1)
            act.activation(scale_T[0:width(IT - 1), IT - 1, :], bank[4][0:width(IT - 1), (IT - 1) * 8:IT * 8], ACT.Copy).then_inc(sT_ready, 1)
            for tile in range(PAIRS):
                act.wait_ge(xT_mm, tile + 1)
                act.activation(xT_hi[:, :, tile * P:(tile + 1) * P], bank[tile % 2][:, :].rearrange("k (g r) -> k g r", g=GH),
                               ACT.Copy).then_inc(xT_hi_ready, 1)
            def open_sum(j, it, m, first):
                n, w = IT * j + it, width(it)
                act.wait_ge(gu_mm, 8 * n + m + 1)
                if not (first and it < 2):
                    act.wait_ge(inter_ready, n - 1)
                act.activation(acc[0:w, it % 3, m, :], gu_bank[m][0:w, :], ACT.Copy,
                               scale=scale_T[0:w, it, 4 * m:4 * m + 1]).then_inc(s0_done, 1)

            def sigmoid(j, it, first):
                n, w = IT * j + it, width(it)
                act.wait_ge(acc_done, 6 * n + 5)
                if not (first and it == 0):
                    act.wait_ge(gs_ready, n)
                act.activation(sig[0:w, :], acc[0:w, it % 3, 0, :], ACT.Sigmoid).then_inc(sig_ready, 1)

            def high_part(j, it, first):
                n, w = IT * j + it, width(it)
                act.wait_ge(inter_ready, n + 1)
                if not (first and it < 2):
                    act.wait_ge(down_mm, projected(*two_units_back(j, it, first)))
                act.activation(in_hi[0:w, it % 3, :], inter[0:w, :], ACT.Copy).then_inc(in_hi_ready, 1)

            def half_precision(j, t):
                act.wait_ge(down_mm, projected(j, IT - 1) - TPC + t + 1)
                act.activation(y16[:, t, :], y_bank[t][:, :], ACT.Copy).then_inc(y16_ready, 1)

            def chunk(j, first):
                for it in range(IT):
                    before = last_unit(j, it, first)
                    evacuate = not first and it == 1
                    if before:
                        sigmoid(*before)
                    if it == 2 and not first:
                        half_precision(j - 1, 3)
                    open_sum(j, it, 0, first)
                    if evacuate:
                        half_precision(j - 1, 0)
                    open_sum(j, it, 1, first)
                    if evacuate:
                        half_precision(j - 1, 1)
                    if before:
                        high_part(*before)
                    if evacuate:
                        half_precision(j - 1, 2)
                    if it == IT - 1 and not first:
                        act.wait_ge(out_ready, TPC * j)
                    if first:
                        act.wait_ge(d_scaled, it + 1)
                        act.activation(wd_hi[0:width(it), it, :], xn[0:width(it), it % 2, :], ACT.Copy).then_inc(d_hi, 1)

            chunk(0, True)
            with act.Fori(1, CHUNKS) as j:
                chunk(j, False)
            sigmoid(CHUNKS - 1, IT - 1, False)
            high_part(CHUNKS - 1, IT - 1, False)
            for t in range(TPC):
                half_precision(CHUNKS - 1, t)

        @block.tensor
        def _(pe):
            pe.wait_ge(s_cast, 1)
            for it in range(IT):
                w = width(it)
                last = pe.transpose(bank[4][0:w, it * 8:(it + 1) * 8], s_rows[:, it * P:it * P + w], ident[0:8, 0:8])
            last.then_inc(sT_mm, 1)
            for tile in range(PAIRS):
                pe.wait_ge(xn_ready, tile + 1)
                if tile >= 2:
                    pe.wait_ge(xT_lo_ready, tile - 1)
                for g in range(GH):
                    last = pe.transpose(bank[tile % 2][:, g * P:(g + 1) * P], xn[:, tile % 2, g * P:(g + 1) * P], ident[:, :])
                last.then_inc(xT_mm, 1)
            pe.wait_ge(sT_ready, 2)
            pe.wait_ge(xT_lo_ready, PAIRS)

            def gate_up(j, it, job, first):
                n, w, (g, m) = IT * j + it, width(it), divmod(job, 2)
                if job < 4:
                    if not (first and it == 0):
                        pe.wait_ge(acc_done, 6 * n - 3 + job)
                elif job < 6:
                    pe.wait_ge(s0_done, 2 * n + job - 3)
                else:
                    pe.wait_ge(acc_done, 6 * n + job - 5)
                lhsT = w_gu[:, m, g, it * P:it * P + w]
                rows = bass.ds(j * CHUNK, CHUNK)
                pe.matmul(gu_bank[job % 4][0:w, :], lhsT, xT_hi[:, g, rows], start=True, stop=False)
                pe.matmul(gu_bank[job % 4][0:w, :], lhsT, xT_lo[:, g, rows], start=False, stop=True).then_inc(gu_mm, 1)

            def down_product(j, it, first, k):
                n, w, buf = IT * j + it, width(it), it % 3
                kind, t = divmod(k, TPC) if it < IT - 1 else (k % 3, k // 3)
                if k == 0:
                    pe.wait_ge(in_hi_ready, n + 1)
                    if first:
                        pe.wait_ge(d_lo, it + 1)
                if it == 0 and not first and kind == 0:
                    pe.wait_ge(y16_ready, TPC * (j - 1) + t + 1)
                if kind == 2 and t == 0:
                    pe.wait_ge(in_lo_ready, n + 1)
                left = (in_hi, in_hi, in_lo)[kind][0:w, buf, t * P:(t + 1) * P]
                right = (wd_hi, wd_lo, wd_hi)[kind][0:w, it, :]
                ins = pe.matmul(y_bank[t][:, :], left, right, start=(it == 0 and kind == 0), stop=(it == IT - 1 and kind == 2))
                if k == 11 or it == IT - 1 and kind == 2:
                    ins.then_inc(down_mm, 1)

            def chunk(j, first):
                for it in range(IT):
                    before = last_unit(j, it, first)
                    before = before and last_unit(*before)
                    k = 0
                    for job in range(8):
                        gate_up(j, it, job, first)
                        while before and k < 12 * (job + 1) // 8:
                            down_product(*before, k)
                            k += 1

            chunk(0, True)
            with pe.Fori(1, CHUNKS) as j:
                chunk(j, False)
            for it in (IT - 2, IT - 1):
                for k in range(12):
                    down_product(CHUNKS - 1, it, False, k)

        @block.vector
        def _(dve):
            dve.wait_ge(rstd_step, 9)
            for tile in range(PAIRS):
                if tile >= 2:
                    dve.wait_ge(xT_mm, tile - 1)
                dve.tensor_scalar(xn[:, tile % 2, :], xall[:, tile, :], ln_work[:, tile, 0:1], rstd[:, tile:tile + 1],
                                  ALU.subtract, ALU.mult).then_inc(xn_ready, 1)
                dve.wait_ge(xT_hi_ready, tile + 1)
                cols = slice(tile * P, (tile + 1) * P)
                dve.tensor_tensor(xT_lo[:, :, cols], bank[tile % 2][:, :].rearrange("k (g r) -> k g r", g=GH),
                                  xT_hi[:, :, cols], ALU.subtract).then_inc(xT_lo_ready, 1)
            dve.wait_ge(tanh_ready, 1)
            dve.wait_ge(sT_ready, 2)

            def add_group(j, it, job):
                n, w, (g, m) = IT * j + it, width(it), divmod(job, 2)
                dve.wait_ge(gu_mm, 8 * n + job + 1)
                if g == 1:
                    dve.wait_ge(s0_done, 2 * n + m + 1)
                else:
                    dve.wait_ge(acc_done, 6 * n + job - 3)
                dve.scalar_tensor_tensor(out=acc[0:w, it % 3, m, :], in0=gu_bank[job % 4][0:w, :],
                                         scalar=scale_T[0:w, it, 4 * m + g:4 * m + g + 1], in1=acc[0:w, it % 3, m, :],
                                         op0=ALU.mult, op1=ALU.add).then_inc(acc_done, 1)

            def activated(j, it, first):
                n, w, buf = IT * j + it, width(it), it % 3
                dve.wait_ge(sig_ready, n + 1)
                if not (first and it == 0):
                    dve.wait_ge(inter_ready, n)
                dve.tensor_tensor(act_gate[0:w, :], acc[0:w, buf, 0, :], sig[0:w, :], ALU.mult).then_inc(gs_ready, 1)
                dve.wait_ge(gs_ready, n + 1)
                dve.wait_ge(acc_done, 6 * n + 6)
                if not (first and it == 0):
                    dve.wait_ge(in_lo_ready, n)
                dve.tensor_tensor(inter[0:w, :], act_gate[0:w, :], acc[0:w, buf, 1, :],
                                  ALU.mult).then_inc(inter_ready, 1)

            def residual(j, t):
                tile = TPC * j + t
                dve.wait_ge(y16_ready, tile + 1)
                dve.scalar_tensor_tensor(out=xall[:, tile, :], in0=y16[:, t, :], scalar=tanh_col[:, 0:1],
                                         in1=xall[:, tile, :], op0=ALU.mult, op1=ALU.add).then_inc(out_ready, 1)

            def scale_down(k):
                w = width(k)
                if k == 0:
                    dve.wait_ge(d_scale_in, 16)
                else:
                    dve.wait_ge(d_lo, k)
                dve.tensor_tensor(xn[0:w, k % 2, :], d_int[0:w, k, :], d_scale[0:w, k, :], ALU.mult).then_inc(d_scaled, 1)

            def low_down(k):
                w = width(k)
                dve.wait_ge(d_hi, k + 1)
                dve.tensor_tensor(wd_lo[0:w, k, :], xn[0:w, k % 2, :], wd_hi[0:w, k, :].bitcast(F32),
                                  ALU.subtract).then_inc(d_lo, 1)

            def chunk(j, first):
                for it in range(IT):
                    before = last_unit(j, it, first)
                    if first:
                        if it:
                            low_down(it - 1)
                        scale_down(it)
                    if before:
                        activated(*before)
                    for job in range(2, 8):
                        add_group(j, it, job)
                    if 3 <= it < 3 + TPC and not first:
                        residual(j - 1, it - 3)

            chunk(0, True)
            low_down(IT - 1)
            with dve.Fori(1, CHUNKS) as j:
                chunk(j, False)
            activated(CHUNKS - 1, IT - 1, False)
            for t in range(TPC):
                residual(CHUNKS - 1, t)


_INS = ["x", "ctx_4096", "g_xattn", "g_ffn", "L0_xattn_Wq", "L0_xattn_Wk", "L0_xattn_Wv", "L0_xattn_Wo", "L0_xattn_bo",
        "L0_xattn_g", "L0_ffn_gate_qweight", "L0_ffn_gate_scales", "L0_ffn_gate_zeros", "L0_ffn_up_qweight",
        "L0_ffn_up_scales", "L0_ffn_up_zeros", "L0_ffn_down_qweight", "L0_ffn_down_scales", "L0_ffn_down_zeros"]


def build(nc, x, ctx, g_xattn, g_ffn, wq, wk, wv, wo, bo, g, gate_q, gate_s, gate_z, up_q, up_s, up_z, down_q, down_s,
          down_z, out):
    with ExitStack() as st:
        xall = st.enter_context(nc.sbuf_tensor("xall", [P, PAIRS, N], F32))
        stats2 = st.enter_context(nc.sbuf_tensor("stats2", [P, PAIRS, 6], F32))
        ident = st.enter_context(nc.sbuf_tensor("ident", [P, P], F32))
        w_gu = st.enter_context(nc.sbuf_tensor("w_gu", [P, 2, GH, INTER], BF16))
        d_int = st.enter_context(nc.sbuf_tensor("d_int", [P, IT, N], BF16))
        gate, up, down = (gate_q, gate_s, gate_z), (up_q, up_s, up_z), (down_q, down_s, down_z)
        attention(nc, x, ctx, g_xattn, wq, wk, wv, wo, bo, g, (gate, up, down), xall, stats2, ident, w_gu, d_int)
        feed_forward(nc, xall, stats2, ident, w_gu, d_int, g_ffn, gate[1], up[1], down[1], out)


def kernel(**inputs):
    import numpy as np
    import concourse.bacc as bacc
    from concourse.bass_utils import run_bass_kernel_spmd

    nc = bacc.Bacc("TRN2", target_bir_lowering=False, num_devices=1)
    arrays, args = {}, []
    for name in _INS:
        a = np.ascontiguousarray(inputs[name])
        arrays[f"in_{name}"] = a
        args.append(nc.dram_tensor(f"in_{name}", a.shape, mybir.dt.from_np(a.dtype), kind="ExternalInput").ap())
    out = nc.dram_tensor("out_x", (BATCH, C, N), F32, kind="ExternalOutput").ap()
    build(nc, *args, out)
    return run_bass_kernel_spmd(nc, [arrays], core_ids=[0]).results[0]["out_x"]
```

```python
from contextlib import ExitStack

import concourse.bass as bass
from concourse import mybir

F32, F32R, BF16, F16, I32 = (mybir.dt.float32, mybir.dt.float32r, mybir.dt.bfloat16, mybir.dt.float16,
                             mybir.dt.int32)
ALU = mybir.AluOpType
ACT = mybir.ActivationFunctionType
AX = mybir.AxisListType

P = 128
BATCH, C, N = 32, 64, 512
HEADS, DH = 8, 64
O = HEADS * DH
OT = O // P
NT = N // P
PAIRS = BATCH // 2
EPS = 1e-5
INTER, GROUP, PACK = 1376, 128, 8
GH = N // GROUP
IT = (INTER + P - 1) // P
ROWS = BATCH * C
CHUNK = 512
CHUNKS = ROWS // CHUNK
TPC = CHUNK // P
XSCALE = 256.0


CONSTS_MADE = 27
WEIGHT_DMAS = 12
DOWNS = 4
assert IT == DOWNS * (PAIRS // 2 - 2 - GH) + 3


def width(it):
    return min(P, INTER - it * P)


def moments(pool, stats, work, inv_counts, half_eps, minus_half, step, before):
    count = [0]

    def tt(out, a, b, op):
        ins = pool.tensor_tensor(out, a, b, op)
        count[0] += 1
        if count[0] <= 7:
            ins.then_inc(step, 1)
            pool.wait_ge(step, before + count[0])
        return ins

    tt(work[..., 2:4], stats[..., 1:3], stats[..., 4:6], ALU.add)
    tt(work[..., 0:2], work[..., 2:4], inv_counts, ALU.mult)
    tt(work[..., 4:5], stats[..., 1:2], stats[..., 4:5], ALU.subtract)
    tt(work[..., 5:6], work[..., 4:5], half_eps[..., 0:1], ALU.mult)
    tt(work[..., 4:5], work[..., 5:6], work[..., 5:6], ALU.mult)
    tt(work[..., 5:6], work[..., 4:5], work[..., 1:2], ALU.add)
    tt(work[..., 6:7], work[..., 5:6], half_eps[..., 1:2], ALU.add)
    return tt(work[..., 7:8], work[..., 6:7], minus_half, ALU.pow)


def attention(nc, x, ctx, g_xattn, wq, wk, wv, wo, bo, g, matrices, xall, stats2, ident, w_gu, d_int,
              ek, ekT, xT_hi, xT_lo, scale_T):
    with ExitStack() as st:
        def sb(name, shape, dt=F32):
            return st.enter_context(nc.sbuf_tensor(name, shape, dt))

        def sem(name):
            return st.enter_context(nc.semaphore(name))

        wq_sb, wk_sb, wv_sb = (ekT[:, 0, s, :].rearrange("p (t a c) -> p t a c", t=OT, a=2) for s in range(3))
        wo_sb = ekT[0:C, 0, 3, :]
        head_of_row = ekT[:, 1, 0:2, :].rearrange("r a (t o) -> r (a t) o", o=P)
        wqT_hi, wqT_lo = sb("wqT_hi", [P, O], F32R), sb("wqT_lo", [P, O], F32R)
        wkT_hi, wkT_lo = sb("wkT_hi", [P, O], F32R), sb("wkT_lo", [P, O], F32R)
        woT = sb("woT", [P, OT, C])
        foldT = sb("foldT", [P, 2, HEADS, C])
        spread = sb("spread", [P, 2 * OT, P], F32R)
        minus_spread = sb("minus_spread", [P, 2 * OT, P], F32R)
        head_sum = sb("head_sum", [P, 2, 32])
        batch_sum = sb("batch_sum", [P, 32])
        minus_half = sb("minus_half", [P, 8])
        ones = sb("ones", [P, 8])
        inv_counts, half_eps = sb("inv_counts", [P, 2]), sb("half_eps", [P, 2])
        bo_col, gate_col, g_col, tanh_col = (sb(n, [P, 1]) for n in ("bo_col", "gate_col", "g_col", "tanh_col"))

        ctx_raw = sb("ctx_raw", [P, 2, N])
        xn = sb("xn", [P, N])
        xs = sb("xs", [P, 2, 2, N], F32R)
        cs = sb("cs", [P, 2, N], F32R)
        stats = sb("stats", [P, 6])
        ln_work = sb("ln_work", [P, 8])
        qmax = sb("qmax", [P, NT, 2, HEADS])
        qmax_rows = sb("qmax_rows", [P, N], F32R)
        kneg = sb("kneg", [P, 2 * OT])
        ksum = sb("ksum", [P, 2 * OT])
        kinv = sb("kinv", [P, 2, 2 * OT])
        eq = sb("eq", [P, 2, 2, OT, N])
        ctxT = sb("ctxT", [P, NT, P])
        den = sb("den", [P, N])
        den_sq = sb("den_sq", [P, C])
        rden = sb("rden", [P, C])
        rden_parts = sb("rden_parts", [P, 2, C], F32R)
        rden_rows = sb("rden_rows", [P, N], F32R)
        kctxT = sb("kctxT", [P, O])
        fold = sb("fold", [P, 2 * OT, C])
        y0 = sb("y0", [P, N])
        ysq = sb("ysq", [P, N])
        ss_rows = sb("ss_rows", [32, N])
        ss_sq = sb("ss_sq", [P, 8])
        ss_max = sb("ss_max", [P, 8])
        rn_sq = sb("rn_sq", [P, 8])
        rn_parts = sb("rn_parts", [P, 2, 8], F32R)
        rn_rows = sb("rn_rows", [P, N], F32R)
        batch_of_row = sb("batch_of_row", [P, P])
        spread_batch = sb("spread_batch", [P, P], F32R)
        yn = sb("yn", [P, N])
        lane = sb("lane", [P, 1], I32)
        nibble = sb("nibble", [P, 1], I32)
        packed = sb("packed", [P, INTER], I32)
        zero = sb("zero", [P, INTER], I32)
        zero_packed = sb("zero_packed", [P, INTER // PACK], I32)
        ln2_work = sb("ln2_work", [P, PAIRS, 8])
        xn2 = ctx_raw
        s_rows16 = zero[0:2 * GH, 0:INTER // 2].bitcast(F16)
        s_rows = packed[0:2 * GH, :].bitcast(F32)

        bank = [st.enter_context(nc.psum_tensor(f"bank{i}", [P, 512], F32)) for i in range(8)]
        dve_ring = bank[0:2]
        k_ring = bank[2:4]
        act_ring = bank[4:6]
        small = bank[6:8]
        drain_ring = bank[2:6]

        weights_in, consts_made, weights_T, wT_ready, fold_mm, fold_ready = (
            sem(n) for n in ("weights_in", "consts_made", "weights_T", "wT_ready", "fold_mm", "fold_ready"))
        gate_parts = sem("gate_parts")
        wT_hi_ready, wT_lo_ready = sem("wT_hi_ready"), sem("wT_lo_ready")
        rden_step, norm_step, ss_bounded, bn2_done, yn_ready, rn_mm = (
            sem(n) for n in ("rden_step", "norm_step", "ss_bounded", "bn2_done", "yn_ready", "rn_mm"))
        loaded = [sem("loaded_even"), sem("loaded_odd")]
        ln_stats, pool_step, rstd_ready, xn_ready = (
            sem(n) for n in ("ln_stats", "pool_step", "rstd_ready", "xn_ready"))
        x_hi, x_lo, c_hi, c_lo = (sem(n) for n in ("x_hi", "x_lo", "c_hi", "c_lo"))
        t_mm, k_mm, q_mm, kt_mm, b_mm = (sem(n) for n in ("t_mm", "k_mm", "q_mm", "kt_mm", "b_mm"))
        t_max, k_max, k_exp, kt_evac, q_exp, q_norm = (
            sem(n) for n in ("t_max", "k_max", "k_exp", "kt_evac", "q_exp", "q_norm"))
        d_mm, a_mm, m_mm, qmaxT_mm, ct_mm, f_mm, ss_mm = (
            sem(n) for n in ("d_mm", "a_mm", "m_mm", "qmaxT_mm", "ct_mm", "f_mm", "ss_mm"))
        d_evac, a_evac, m_evac, qmaxT_evac, ct_evac, y_evac, ss_evac = (
            sem(n) for n in ("d_evac", "a_evac", "m_evac", "qmaxT_evac", "ct_evac", "y_evac", "ss_evac"))
        kinv_ready, rden_ready, rn_ready, x1_done = (
            sem(n) for n in ("kinv_ready", "rden_ready", "rn_ready", "x1_done"))
        den_spread, rden_gathered, ss_spread, rn_gathered = (
            sem(n) for n in ("den_spread", "rden_gathered", "ss_spread", "rn_gathered"))

        scales_in, s_cast, sT_mm, sT_ready = sem("scales_in"), sem("s_cast"), sem("sT_mm"), sem("sT_ready")
        ln2_step, xn2_ready, xT_mm, xT_hi_ready, xT_lo_ready = (
            sem(n) for n in ("ln2_step", "xn2_ready", "xT_mm", "xT_hi_ready", "xT_lo_ready"))
        zeros_in, packed_in = sem("zeros_in"), sem("packed_in")
        zero_ready, nib, w_int = sem("zero_ready"), sem("nib"), sem("w_int")

        ln2_parts = [(0, PAIRS - 4), (PAIRS - 4, 2), (PAIRS - 2, 1), (PAIRS - 1, 1)]

        def unpacked_in(p, kind):
            if kind < 2:
                return 16 * (p - 1)
            return 16 * (2 * GH + 2 * (p - 1 - 2 * GH) - (1 if isinstance(p, int) and p == PAIRS - 1 else 0))

        block = st.enter_context(nc.Block())

        x_rows = x.rearrange("(p two) c n -> p (two c) n", two=2)
        ctx_rows = ctx.rearrange("(p two) c n -> p (two c) n", two=2)

        def masks_made(eng):
            eng.wait_ge(consts_made, CONSTS_MADE)

        @block.sync
        def _(sp):
            def load(p, half, par):
                sp.dma_start(xall[:, p, :], x_rows[p]).then_inc(loaded[par], 16)
                sp.dma_start(ctx_raw[:, par, :], ctx_rows[p]).then_inc(loaded[par], 16)

            def row(ap):
                return ap.rearrange("(c one) -> c one", one=1)

            for w, dst in ((wq, wq_sb), (wk, wk_sb), (wv, wv_sb)):
                for twice in range(2):
                    sp.dma_start(dst[:, :, twice, :], w.rearrange("(t p) c -> p t c", p=P)).then_inc(weights_in, 16)
            sp.dma_start(wo_sb[:, :], wo).then_inc(weights_in, 16)
            load(0, 0, 0)
            load(1, 0, 1)
            for b in range(2):
                half = slice(b * C, (b + 1) * C)
                sp.dma_start(bo_col[half, :], row(bo)).then_inc(weights_in, 16)
                sp.dma_start(g_col[half, :], g.rearrange("one c two -> (one c) two")).then_inc(weights_in, 16)
            sp.dma_start(tanh_col[:, :], row(g_xattn).to_broadcast([P, 1])).then_inc(weights_in, 16)

            def step(p, i, par, project, combine, residual):
                if combine:
                    r = p - 1
                    sp.wait_ge(d_evac, r + 1)
                    for grp in range(4):
                        sp.dma_start(den_sq[32 * grp:32 * grp + 32, :],
                                     den[32 * grp:32 * grp + 4, :].rearrange("h (k m) -> h k m", m=C)
                                     ).then_inc(den_spread, 16)
                    sp.wait_ge(rden_ready, r + 1)
                    for part in range(2):
                        sp.dma_start(rden_rows[16 * part:16 * part + 16, :].bitcast(F32).rearrange("r (k m) -> r k m", m=C),
                                     rden_parts[:, part, :].bitcast(F32)).then_inc(rden_gathered, 16)
                if residual:
                    r2 = p - 2
                    sp.wait_ge(ss_evac, r2 + 1)
                    sp.dma_start(ss_sq[:, :],
                                 ss_rows[0:2, :].rearrange("b (k m) -> b k m", m=8)).then_inc(ss_spread, 16)
                    sp.wait_ge(rn_ready, 2 * r2 + 2)
                    for part in range(2):
                        sp.dma_start(rn_rows[2 * part:2 * part + 2, :].bitcast(F32).rearrange("b (k m) -> b k m", m=8),
                                     rn_parts[:, part, :].bitcast(F32)).then_inc(rn_gathered, 16)

            def load_weights(p, kind, k, count):
                qweight, _, zeros = matrices[kind]
                cols = qweight.shape[1]
                rows = width(k) if kind == 2 and isinstance(k, int) else P
                if not (isinstance(p, int) and p == 2):
                    sp.wait_ge(w_int, p - 2)
                sp.dma_start(zero_packed[:, 0:count * cols // PACK],
                             zeros[bass.ds(k, count), :].rearrange("g w -> (g w)").partition_broadcast(P)
                             ).then_inc(zeros_in, 16)
                for c in range(count):
                    words = qweight[bass.ds((k + c) * (GROUP // PACK), rows // PACK), :]
                    sp.dma_start(packed[0:rows, c * cols:(c + 1) * cols],
                                 words.unsqueeze(1).to_broadcast([rows // PACK, PACK, cols])).then_inc(packed_in, 16)

            def step_and_load(p, i, par, project, combine, residual, weights=None):
                if weights:
                    load_weights(p, *weights)
                step(p, i, par, project, combine, residual)
                sp.wait_ge(ct_mm, p + 1)
                load(p + 2, i + 1, par)

            step_and_load(0, 0, 0, True, False, False)
            step_and_load(1, 0, 1, True, True, False)
            with sp.Fori(1, GH + 1) as i:
                step_and_load(2 * i, i, 0, True, True, True, (0, i - 1, 1))
                step_and_load(2 * i + 1, i, 1, True, True, True, (1, i - 1, 1))
            with sp.Fori(GH + 1, PAIRS // 2 - 1) as i:
                step_and_load(2 * i, i, 0, True, True, True, (2, DOWNS * i - DOWNS * (GH + 1), 2))
                step_and_load(2 * i + 1, i, 1, True, True, True, (2, DOWNS * i - DOWNS * (GH + 1) + 2, 2))
            load_weights(PAIRS - 2, 2, IT - 3, 2)
            step(PAIRS - 2, 0, 0, True, True, True)
            load_weights(PAIRS - 1, 2, IT - 1, 1)
            step(PAIRS - 1, 0, 1, True, True, True)
            sp.wait_ge(w_int, PAIRS - 2)
            for m in range(2):
                sp.dma_start(s_rows16[m * GH:(m + 1) * GH, :], matrices[m][1]).then_inc(scales_in, 16)
            step(PAIRS, 0, 0, False, True, True)
            step(PAIRS + 1, 0, 1, False, False, True)

        @block.gpsimd
        def _(pool):
            made = [0]

            def then(ins):
                made[0] += 1
                ins.then_inc(consts_made, 1)
                pool.wait_ge(consts_made, made[0])

            then(pool.iota(lane[:, :], [[0, 1]], base=0, channel_multiplier=4))
            then(pool.memset(ident[:, :], 0.0))
            then(pool.memset(head_of_row[:, :, :], 0.0))
            then(pool.memset(head_sum[:, :, :], 0.0))
            then(pool.memset(foldT[:, :, :, :], 0.0))
            then(pool.memset(batch_sum[:, :], 0.0))
            then(pool.memset(minus_half[:, :], -0.5))
            then(pool.memset(ones[:, :], 1.0))
            then(pool.memset(inv_counts[:, 0:1], 0.5))
            then(pool.memset(inv_counts[:, 1:2], 1.0 / N))
            then(pool.memset(half_eps[:, 0:1], 0.5))
            then(pool.memset(half_eps[:, 1:2], EPS))
            then(pool.memset(qmax_rows[:, :].bitcast(F32), 0.0))
            then(pool.memset(rden_rows[:, :].bitcast(F32), 0.0))
            then(pool.memset(rn_rows[:, :].bitcast(F32), 0.0))
            then(pool.memset(batch_of_row[:, :], 0.0))
            then(pool.affine_select(out=ident[:, :], in_=ident[:, :], compare_op=ALU.not_equal, fill=1.0, base=0,
                                    pattern=[[-1, P]], channel_multiplier=1))
            rows = head_of_row[:, :, :].rearrange("r bt (e d) -> r bt e d", e=2)
            for part in range(2):
                then(pool.affine_select(out=rows, in_=rows, compare_op=ALU.not_equal, fill=1.0, base=-16 * part,
                                        pattern=[[-2, 2 * OT], [-1, 2], [0, DH]], channel_multiplier=1))
            rows = batch_of_row[:, :].rearrange("r (b c) -> r b c", b=2)
            for part in range(2):
                then(pool.affine_select(out=rows, in_=rows, compare_op=ALU.not_equal, fill=1.0, base=-2 * part,
                                        pattern=[[-1, 2], [0, C]], channel_multiplier=1))
            for e in range(2):
                half = slice(e * DH, (e + 1) * DH)
                for tt in range(2):
                    then(pool.memset(head_sum[half, tt, :].rearrange("o (m f) -> o m f", f=4)[:, :, 2 * tt + e],
                                     float(DH) ** 0.5))
                then(pool.memset(batch_sum[half, :].rearrange("o (m f) -> o m f", f=2)[:, :, e], 1.0))
            assert made[0] == CONSTS_MADE

            def layernorm(p):
                pool.wait_ge(ln_stats, p + 1)
                moments(pool, stats[:, :], ln_work[:, :], inv_counts[:, :], half_eps[:, :], minus_half[:, 0:1], pool_step,
                        7 * p).then_inc(rstd_ready, 1)
                pool.wait_ge(rstd_ready, p + 1)

            def inverse_norm(r):
                pool.wait_ge(ss_bounded, r + 1)
                pool.tensor_tensor(rn_sq[:, :], ss_max[:, :], minus_half[:, :], ALU.pow).then_inc(norm_step, 1)
                pool.wait_ge(norm_step, r + 1)
                pool.tensor_tensor(rn_parts[:, 0, :], rn_sq[:, :], ones[:, :], ALU.mult).then_inc(rn_ready, 1)
                pool.wait_ge(rn_ready, 2 * r + 1)
                pool.tensor_tensor(rn_parts[:, 1, :], rn_sq[:, :], rn_parts[:, 0, :].bitcast(F32),
                                   ALU.subtract).then_inc(rn_ready, 1)
                pool.wait_ge(rn_ready, 2 * r + 2)

            def low_parts(p, hi_ready, raw, split, lo_ready):
                for b in range(2):
                    rows, other = slice(b * C, (b + 1) * C), slice((1 - b) * C, (2 - b) * C)
                    pool.wait_ge(hi_ready, 2 * p + b + 1)
                    pool.tensor_tensor(split[other, b, :], raw[rows], split[rows, b, :].bitcast(F32),
                                       ALU.subtract).then_inc(lo_ready, 1)
                    pool.wait_ge(lo_ready, 2 * p + b + 1)

            def step(p, par, residual, following=True):
                if following:
                    layernorm(p + 1)
                    low_parts(p + 1, c_hi, ctx_raw[:, 1 - par, :], cs, c_lo)
                if residual:
                    inverse_norm(p - 2)
                if following:
                    low_parts(p + 1, x_hi, xn[:, :], xs[:, 1 - par], x_lo)

            pool.wait_ge(consts_made, made[0])
            layernorm(0)
            low_parts(0, c_hi, ctx_raw[:, 0, :], cs, c_lo)
            low_parts(0, x_hi, xn[:, :], xs[:, 0], x_lo)
            step(0, 0, False)
            step(1, 1, False)
            with pool.Fori(1, PAIRS // 2 - 1) as i:
                step(2 * i, 0, True)
                step(2 * i + 1, 1, True)
            step(PAIRS - 2, 0, True)

            def second_moments(part):
                first, count = ln2_parts[part]
                before, work = 9 * part, ln2_work[:, first:first + count, :]
                pool.wait_ge(bn2_done, first + count)
                moments(pool, stats2[:, first:first + count, :], work, inv_counts[:, :].unsqueeze(1).to_broadcast([P, count, 2]),
                        half_eps[:, :].unsqueeze(1).to_broadcast([P, count, 2]),
                        minus_half[:, 0:1].unsqueeze(1).to_broadcast([P, count, 1]), ln2_step, before).then_inc(ln2_step, 1)
                pool.wait_ge(ln2_step, before + 8)
                pool.tensor_scalar(work[..., 6:7], work[..., 7:8], XSCALE, None, ALU.mult).then_inc(ln2_step, 1)
                pool.wait_ge(ln2_step, before + 9)

            second_moments(0)
            step(PAIRS - 1, 1, True, False)
            second_moments(1)
            step(PAIRS, 0, True, False)
            second_moments(2)
            step(PAIRS + 1, 1, True, False)
            second_moments(3)

        def k_slot(b, t):
            return b * OT + t

        @block.scalar
        def _(act):
            act.wait_ge(weights_T, 1)
            act.activation(wqT_hi[:, :], bank[0][:, :], ACT.Copy).then_inc(wT_hi_ready, 1)
            act.wait_ge(weights_T, 2)
            act.activation(wkT_hi[:, :], bank[1][:, :], ACT.Copy, scale=-1.0).then_inc(wT_hi_ready, 1)
            act.wait_ge(weights_T, 3)
            act.activation(woT[:, :, :].rearrange("p t c -> p (t c)"), bank[2][:, 0:OT * C], ACT.Copy).then_inc(wT_ready, 1)
            act.wait_ge(consts_made, CONSTS_MADE)
            act.activation(spread[:, :, :], head_of_row[:, :, :], ACT.Copy).then_inc(wT_ready, 1)
            act.activation(spread_batch[:, :], batch_of_row[:, :], ACT.Copy).then_inc(wT_ready, 1)
            act.activation(minus_spread[:, :, :], head_of_row[:, :, :], ACT.Copy, scale=-1.0).then_inc(wT_ready, 1)
            act.wait_ge(fold_mm, 1)
            for b in range(2):
                rows = slice(b * C, (b + 1) * C)
                for e in range(2):
                    act.activation(foldT[rows, b, e::2, :], bank[3 + e][rows, :].rearrange("c (h d) -> c h d", d=C)[:, e::2, :],
                                   ACT.Copy).then_inc(fold_ready, 1)
            act.wait_ge(weights_in, 16 * WEIGHT_DMAS)
            act.activation(tanh_col[:, :], tanh_col[:, :], ACT.Tanh).then_inc(gate_parts, 1)

            def ctx_high(p, half, par):
                act.wait_ge(loaded[par], 32 * (half + 1))
                for b in range(2):
                    rows = slice(b * C, (b + 1) * C)
                    act.activation(cs[rows, b, :], ctx_raw[rows, par, :], ACT.Copy).then_inc(c_hi, 1)

            def x_high(p, par):
                act.wait_ge(xn_ready, p + 1)
                for b in range(2):
                    rows = slice(b * C, (b + 1) * C)
                    act.activation(xs[rows, par, b, :], xn[rows, :], ACT.Copy).then_inc(x_hi, 1)

            ctx_high(0, 0, 0)
            x_high(0, 0)

            def step(p, i, par, project, combine, residual, last=False, drain=False):
                r = p - 1
                first = isinstance(p, int) and p == 0

                def k_exp_tile(b, t):
                    n = 8 * p + b * OT + t
                    act.wait_ge(k_max, n + 1)
                    if t == 0 and not first:
                        act.wait_ge(kt_mm, 8 * p - 4 + 4 * b)
                        if b == 0:
                            act.wait_ge(kinv_ready, p)
                    act.activation(ek[:, b, t, :], k_ring[t % 2][:, :], ACT.Exp, bias=kneg[:, k_slot(b, t):k_slot(b, t) + 1],
                                   scale=-1.0, accum_out=ksum[:, k_slot(b, t):k_slot(b, t) + 1]).then_inc(k_exp, 1)

                def k_transposed(b, t):
                    act.wait_ge(kt_mm, 8 * p + 4 * b + t + 1)
                    act.activation(ekT[:, b, t, :], act_ring[t % 2][:, :], ACT.Copy).then_inc(kt_evac, 1)

                def q_exp_tile(b, t):
                    act.wait_ge(q_mm, 8 * p + 4 * b + t + 1)
                    act.activation(eq[:, par, b, t, :], act_ring[t % 2][:, :], ACT.Exp).then_inc(q_exp, 1)

                if project:
                    k_exp_tile(0, 0)
                if combine:
                    act.wait_ge(d_mm, r + 1)
                    act.activation(den[:, :], small[0][:, :], ACT.Copy).then_inc(d_evac, 1)
                if drain and combine:
                    act.wait_ge(scales_in, 32)
                    act.activation(s_rows, s_rows16, ACT.Copy, scale=1.0 / XSCALE).then_inc(s_cast, 1)
                    transposed(0, 2)
                if project:
                    for t in range(1, OT):
                        k_exp_tile(0, t)
                    k_exp_tile(1, 0)
                    k_exp_tile(1, 1)
                if combine:
                    act.wait_ge(a_mm, r + 1)
                    act.activation(kctxT[:, :], small[1][:, :], ACT.Copy).then_inc(a_evac, 1)
                if drain and combine:
                    transposed(2, 3)
                    act.wait_ge(sT_mm, 1)
                    sT = drain_ring[3]
                    act.activation(scale_T[:, 0:IT - 1, :].rearrange("p i s -> p (i s)"), sT[:, 0:(IT - 1) * 8],
                                   ACT.Copy).then_inc(sT_ready, 1)
                    act.activation(scale_T[0:width(IT - 1), IT - 1, :], sT[0:width(IT - 1), (IT - 1) * 8:IT * 8],
                                   ACT.Copy).then_inc(sT_ready, 1)
                    transposed(3, 6)
                if project:
                    k_exp_tile(1, 2)
                    k_exp_tile(1, 3)
                    for t in range(3):
                        k_transposed(0, t)
                    act.wait_ge(qmaxT_mm, p + 1)
                    act.activation(qmax_rows[0:16, :], small[0][0:16, :], ACT.Copy).then_inc(qmaxT_evac, 1)
                if residual:
                    act.wait_ge(f_mm, r)
                    act.activation(y0[:, :], small[1][:, :], ACT.Identity, bias=bo_col[:, 0:1]).then_inc(y_evac, 1)
                    act.activation(ysq[:, :], small[1][:, :], ACT.Square, bias=bo_col[:, 0:1]).then_inc(y_evac, 1)
                if drain:
                    transposed(*((6, 8) if combine else (12, 14)))
                if project:
                    k_transposed(0, 3)
                    if not last:
                        act.wait_ge(k_mm, 8 * p + 8)
                        ctx_high(p + 1, i + par, 1 - par)
                    q_exp_tile(0, 0)
                    q_exp_tile(0, 1)
                if residual:
                    act.wait_ge(ss_mm, r)
                    act.activation(ss_rows[:, :], small[0][0:32, :], ACT.Copy).then_inc(ss_evac, 1)
                if project:
                    q_exp_tile(0, 2)
                    q_exp_tile(0, 3)
                    for t in range(NT):
                        k_transposed(1, t)
                    if not last:
                        x_high(p + 1, 1 - par)
                    for t in range(OT):
                        q_exp_tile(1, t)
                    act.wait_ge(ct_mm, p + 1)
                    act.activation(ctxT[:, :, :].rearrange("n t c -> n (t c)"), small[0][:, :], ACT.Copy).then_inc(ct_evac, 1)
                if drain:
                    transposed(*((8, 12) if combine else (14, 16)))
                if residual:
                    act.wait_ge(yn_ready, r)

            def transposed(first, end):
                for k in range(first, end):
                    act.wait_ge(xT_mm, k + 1)
                    act.activation(xT_hi[:, :, k * P:(k + 1) * P], drain_ring[k % 4][:, :].rearrange("k (g r) -> k g r", g=GH),
                                   ACT.Copy).then_inc(xT_hi_ready, 1)

            step(0, 0, 0, True, False, False)
            step(1, 0, 1, True, True, False)
            with act.Fori(1, PAIRS // 2 - 1) as i:
                step(2 * i, i, 0, True, True, True)
                step(2 * i + 1, i, 1, True, True, True)
            step(PAIRS - 2, PAIRS // 2 - 1, 0, True, True, True)
            step(PAIRS - 1, PAIRS // 2 - 1, 1, True, True, True, last=True)
            step(PAIRS, PAIRS // 2, 0, False, True, True, drain=True)
            step(PAIRS + 1, PAIRS // 2, 1, False, False, True, drain=True)

        @block.tensor
        def _(pe):
            pe.wait_ge(consts_made, CONSTS_MADE)
            pe.wait_ge(weights_in, 16 * WEIGHT_DMAS)
            for w, ps in ((wq_sb, bank[0]), (wk_sb, bank[1])):
                for t in range(OT):
                    last = pe.transpose(ps[:, t * P:(t + 1) * P], w[:, t, :, :].rearrange("p a c -> p (a c)"), ident[:, :])
                last.then_inc(weights_T, 1)
            for t in range(OT):
                last = pe.transpose(bank[2][:, t * C:(t + 1) * C], wo_sb[:, t * P:(t + 1) * P], ident[0:C, 0:C])
            last.then_inc(weights_T, 1)
            pe.wait_ge(wT_ready, 1)
            for h in range(HEADS):
                rows = slice((h % 2) * DH, (h % 2 + 1) * DH)
                last = pe.matmul(bank[3 + h % 2][:, h * C:(h + 1) * C], wv_sb[rows, h // 2, :, :].rearrange("p a c -> p (a c)"),
                                 woT[rows, h // 2, :], start=True, stop=True)
            last.then_inc(fold_mm, 1)
            pe.wait_ge(wT_ready, 4)
            pe.wait_ge(wT_lo_ready, 2)
            pe.wait_ge(fold_ready, 4)

            def step(p, i, par, project, combine, residual, drain=False):
                r = p - 1
                first = isinstance(p, int) and p == 0
                qpar = 1 - par

                def t_and_k(b, t):
                    if not project:
                        return
                    n = 8 * p + 4 * b + t
                    if b == 0 and t < 2:
                        if residual:
                            pe.wait_ge(q_norm, 8 * r - 1 + t)
                    else:
                        pe.wait_ge(t_max, n - 1)
                    if t == 0:
                        pe.wait_ge(x_lo, 2 * p + b + 1)
                    pe.matmul(dve_ring[t % 2][:, :], xs[:, par, b, t * P:(t + 1) * P], wqT_hi[:, :],
                              start=True, stop=True).then_inc(t_mm, 1)
                    if not (first and b == 0 and t < 2):
                        pe.wait_ge(k_exp, n - 1)
                    if t == 0:
                        pe.wait_ge(c_lo, 2 * p + b + 1)
                    pe.matmul(k_ring[t % 2][:, :], wkT_hi[:, t * P:(t + 1) * P], cs[:, b, :], start=True, stop=False)
                    pe.matmul(k_ring[t % 2][:, :], wkT_lo[:, t * P:(t + 1) * P], cs[:, b, :],
                              start=False, stop=True).then_inc(k_mm, 1)

                def denominators(tt):
                    if not combine:
                        return
                    if tt == 0:
                        pe.wait_ge(q_exp, 8 * r + 8)
                        pe.wait_ge(ct_evac, r + 1)
                    for grp in range(4):
                        b, t = grp // 2, 2 * (grp % 2) + tt
                        last = pe.matmul(small[0][32 * grp:32 * grp + 32, :], head_sum[:, tt, :], eq[:, qpar, b, t, :],
                                         start=(tt == 0), stop=(tt == 1))
                    if tt == 1:
                        last.then_inc(d_mm, 1)

                def context(t):
                    if not combine:
                        return
                    if t == 0:
                        pe.wait_ge(kt_evac, 8 * r + 8)
                        pe.wait_ge(ct_evac, r + 1)
                        if residual:
                            pe.wait_ge(m_evac, r)
                    for b in range(2):
                        last = pe.matmul(small[1][b * C:(b + 1) * C, :], ctxT[:, t, b * C:(b + 1) * C], ekT[:, b, t, :],
                                         start=(t == 0), stop=(t == NT - 1))
                    if t == NT - 1:
                        last.then_inc(a_mm, 1)

                def q_max_rows():
                    if not project:
                        return
                    pe.wait_ge(t_max, 8 * p + 8)
                    if combine:
                        pe.wait_ge(d_evac, r + 1)
                    for t in range(NT):
                        last = pe.transpose(small[0][0:16, t * P:(t + 1) * P],
                                            qmax[:, t, :, :].rearrange("n b h -> n (b h)"), ident[:, :])
                    last.then_inc(qmaxT_mm, 1)

                def act_ring_free(kind, b, t):
                    if t >= 2:
                        pe.wait_ge(kt_evac if kind == "kt" else q_exp, 8 * p + 4 * b + t - 1)
                    elif kind == "q":
                        pe.wait_ge(kt_evac, 8 * p + 4 * b + t + 3)
                    elif b == 1:
                        pe.wait_ge(q_exp, 8 * p + t + 3)
                    elif not first:
                        pe.wait_ge(q_exp, 8 * p - 1 + t)

                def k_transposed(b, t):
                    if not project:
                        return
                    act_ring_free("kt", b, t)
                    if t == 0:
                        pe.wait_ge(k_exp, 8 * p + 4 * b + 4)
                    for ot in range(OT):
                        last = pe.transpose(act_ring[t % 2][:, ot * P:(ot + 1) * P], ek[:, b, ot, t * P:(t + 1) * P], ident[:, :])
                    last.then_inc(kt_mm, 1)

                def q_logits(b, t):
                    if not project:
                        return
                    act_ring_free("q", b, t)
                    if b == 0 and t == 0:
                        pe.wait_ge(qmaxT_evac, p + 1)
                    out, cols = act_ring[t % 2][:, :], slice(t * P, (t + 1) * P)
                    pe.matmul(out, wqT_hi[:, cols], xs[:, par, b, :], start=True, stop=False)
                    pe.matmul(out, wqT_lo[:, cols], xs[:, par, b, :], start=False, stop=False)
                    pe.matmul(out, minus_spread[:, k_slot(b, t), :], qmax_rows[:, :], start=False,
                              stop=True).then_inc(q_mm, 1)

                def fold_context():
                    if not combine:
                        return
                    pe.wait_ge(a_evac, r + 1)
                    if residual:
                        pe.wait_ge(y_evac, 2 * r)
                    for b in range(2):
                        for t in range(OT):
                            for e in range(2):
                                last = pe.matmul(small[1][e * DH:(e + 1) * DH, k_slot(b, t) * C:(k_slot(b, t) + 1) * C],
                                                 kctxT[:, t * P + e * DH:t * P + (e + 1) * DH],
                                                 foldT[:, b, 2 * t + e, :], start=True, stop=True)
                    last.then_inc(m_mm, 1)

                def spread_reciprocals(b, t):
                    if not combine:
                        return
                    n = 8 * r + 4 * b + t
                    if b == 0 and t == 0:
                        pe.wait_ge(rden_gathered, 32 * (r + 1))
                    if b == 0 and t < 2 and project:
                        pe.wait_ge(t_max, 8 * p + 8)
                    else:
                        pe.wait_ge(q_norm, n - 1)
                    pe.matmul(dve_ring[t % 2][:, :], spread[:, k_slot(b, t), :], rden_rows[:, :],
                              start=True, stop=True).then_inc(b_mm, 1)

                def ctx_transposed():
                    if not project:
                        return
                    pe.wait_ge(loaded[par], 32 * (i + 1))
                    pe.wait_ge(qmaxT_evac, p + 1)
                    if residual:
                        pe.wait_ge(ss_evac, r)
                    for t in range(NT):
                        last = pe.transpose(small[0][:, t * P:(t + 1) * P], ctx_raw[:, par, t * P:(t + 1) * P], ident[:, :])
                    last.then_inc(ct_mm, 1)

                def spread_inverse_norm():
                    if not residual:
                        return
                    pe.wait_ge(rn_gathered, 32 * (r - 1) + 32)
                    if combine:
                        pe.wait_ge(m_evac, r + 1)
                    else:
                        pe.wait_ge(y_evac, 2 * r)
                    pe.matmul(small[1][:, :], spread_batch[:, :], rn_rows[:, :], start=True, stop=True).then_inc(rn_mm, 1)

                def output(t):
                    if not residual:
                        return
                    if t == 0:
                        pe.wait_ge(q_norm, 8 * r)
                        pe.wait_ge(m_evac, r)
                        if combine:
                            pe.wait_ge(a_evac, r + 1)
                    for b in range(2):
                        last = pe.matmul(small[1][b * C:(b + 1) * C, :], fold[:, k_slot(b, t), :], eq[:, par, b, t, :],
                                         start=(t == 0), stop=(t == OT - 1))
                    if t == OT - 1:
                        last.then_inc(f_mm, 1)

                def squared_norms():
                    if not residual:
                        return
                    pe.wait_ge(y_evac, 2 * r)
                    if project:
                        pe.wait_ge(qmaxT_evac, p + 1)
                    elif combine:
                        pe.wait_ge(d_evac, r + 1)
                    else:
                        pe.wait_ge(ss_evac, r - 1)
                    pe.matmul(small[0][0:32, :], batch_sum[:, :], ysq[:, :], start=True, stop=True).then_inc(ss_mm, 1)

                def ffn_input(*tiles):
                    for k in tiles:
                        if k == 3:
                            pe.wait_ge(s_cast, 1)
                            for it in range(IT):
                                w = width(it)
                                last = pe.transpose(drain_ring[3][0:w, it * 8:(it + 1) * 8], s_rows[:, it * P:it * P + w],
                                                    ident[0:8, 0:8])
                            last.then_inc(sT_mm, 1)
                            pe.wait_ge(sT_ready, 2)
                        if k >= 4:
                            pe.wait_ge(xT_lo_ready, k - 3)
                        pe.wait_ge(xn2_ready, k + 1)
                        for g in range(GH):
                            last = pe.transpose(drain_ring[k % 4][:, g * P:(g + 1) * P], xn2[:, k % 2, g * P:(g + 1) * P],
                                                ident[:, :])
                        last.then_inc(xT_mm, 1)

                if drain:
                    if combine:
                        denominators(0)
                        denominators(1)
                        ffn_input(0)
                        ffn_input(1)
                        context(0)
                        context(1)
                        context(2)
                        context(3)
                        ffn_input(2)
                        ffn_input(3)
                        output(0)
                        output(1)
                        output(2)
                        output(3)
                        ffn_input(4)
                        ffn_input(5)
                        ffn_input(6)
                        ffn_input(7)
                        squared_norms()
                        fold_context()
                        spread_reciprocals(0, 0)
                        spread_reciprocals(0, 1)
                        spread_reciprocals(0, 2)
                        spread_reciprocals(0, 3)
                        ffn_input(8)
                        spread_reciprocals(1, 0)
                        spread_reciprocals(1, 1)
                        ffn_input(9)
                        spread_reciprocals(1, 2)
                        spread_reciprocals(1, 3)
                        ffn_input(10)
                        ffn_input(11)
                        spread_inverse_norm()
                    else:
                        output(0)
                        output(1)
                        output(2)
                        output(3)
                        ffn_input(12)
                        ffn_input(13)
                        squared_norms()
                        ffn_input(14)
                        spread_inverse_norm()
                        ffn_input(15)
                    return
                t_and_k(0, 0)
                denominators(0)
                denominators(1)
                t_and_k(0, 1)
                context(0)
                t_and_k(0, 2)
                t_and_k(0, 3)
                context(1)
                t_and_k(1, 0)
                context(2)
                t_and_k(1, 1)
                context(3)
                t_and_k(1, 2)
                t_and_k(1, 3)
                output(0)
                k_transposed(0, 0)
                output(1)
                k_transposed(0, 1)
                output(2)
                k_transposed(0, 2)
                q_max_rows()
                output(3)
                k_transposed(0, 3)
                q_logits(0, 0)
                q_logits(0, 1)
                squared_norms()
                fold_context()
                spread_reciprocals(0, 0)
                q_logits(0, 2)
                spread_reciprocals(0, 1)
                q_logits(0, 3)
                spread_reciprocals(0, 2)
                k_transposed(1, 0)
                spread_reciprocals(0, 3)
                k_transposed(1, 1)
                spread_reciprocals(1, 0)
                k_transposed(1, 2)
                spread_reciprocals(1, 1)
                k_transposed(1, 3)
                spread_reciprocals(1, 2)
                q_logits(1, 0)
                spread_reciprocals(1, 3)
                q_logits(1, 1)
                spread_inverse_norm()
                q_logits(1, 2)
                q_logits(1, 3)
                ctx_transposed()
                if residual:
                    pe.wait_ge(yn_ready, r)

            step(0, 0, 0, True, False, False)
            step(1, 0, 1, True, True, False)
            with pe.Fori(1, PAIRS // 2) as i:
                step(2 * i, i, 0, True, True, True)
                step(2 * i + 1, i, 1, True, True, True)
            pe.wait_ge(kt_evac, 8 * PAIRS)
            pe.wait_ge(q_exp, 8 * PAIRS)
            step(PAIRS, PAIRS // 2, 0, False, True, True, drain=True)
            pe.wait_ge(yn_ready, PAIRS - 1)
            step(PAIRS + 1, PAIRS // 2, 1, False, False, True, drain=True)

        @block.vector
        def _(dve):
            for n, (ps, hi, lo, sign) in enumerate(((bank[0], wqT_hi, wqT_lo, 1.0), (bank[1], wkT_hi, wkT_lo, -1.0))):
                dve.wait_ge(wT_hi_ready, n + 1)
                dve.scalar_tensor_tensor(out=lo[:, :], in0=ps[:, :], scalar=sign, in1=hi[:, :].bitcast(F32), op0=ALU.mult,
                                         op1=ALU.subtract).then_inc(wT_lo_ready, 1)
            dve.wait_ge(gate_parts, 1)
            dve.tensor_scalar(gate_col[:, :], g_col[:, :], tanh_col[:, 0:1], float(C) ** 0.5, ALU.mult,
                              ALU.mult).then_inc(gate_parts, 1)

            dve.wait_ge(gate_parts, 2)
            dve.wait_ge(consts_made, CONSTS_MADE)
            dve.tensor_scalar(nibble[:, :], lane[:, :], 31, None, ALU.bitwise_and).then_inc(nib, 1)

            def unpack(p, kind, k, count):
                cols = count * matrices[kind][0].shape[1]
                rows = width(k) if kind == 2 and isinstance(k, int) else P
                dve.wait_ge(zeros_in, 16 * (p - 1))
                if not (isinstance(p, int) and p == 2):
                    dve.wait_ge(w_int, p - 2)
                for e in range(PACK):
                    last = dve.tensor_scalar(zero[:, 0:cols].rearrange("p (w e) -> p w e", e=PACK)[:, :, e],
                                             zero_packed[:, 0:cols // PACK], 4 * e, 15,
                                             ALU.logical_shift_right, ALU.bitwise_and)
                last.then_inc(zero_ready, 1)
                word, z = packed[0:rows, 0:cols], zero[0:rows, 0:cols]
                dve.wait_ge(packed_in, unpacked_in(p, kind))
                dve.tensor_scalar(word, word, nibble[0:rows, 0:1], 15, ALU.logical_shift_right,
                                  ALU.bitwise_and).then_inc(nib, 1)
                dve.wait_ge(nib, p)
                dve.wait_ge(zero_ready, p - 1)
                if kind == 2:
                    out = d_int[0:rows, bass.ds(k, count), :]
                    word, z = (a.rearrange("p (g n) -> p g n", g=count) for a in (word, z))
                else:
                    out = w_gu[:, kind, bass.ds(k, 1), :]
                    word, z = word.unsqueeze(1), z.unsqueeze(1)
                dve.scalar_tensor_tensor(out=out, in0=word, scalar=1.0, in1=z, op0=ALU.subtract,
                                         op1=ALU.subtract).then_inc(w_int, 1)

            def layernorm_stats(p, half, par):
                masks_made(dve)
                dve.wait_ge(loaded[par], 32 * (half + 1))
                if not (isinstance(p, int) and p == 0):
                    dve.wait_ge(rstd_ready, p)
                dve.bn_stats(stats[:, :], xall[:, p, :]).then_inc(ln_stats, 1)

            def layernorm_apply(p):
                dve.wait_ge(rstd_ready, p + 1)
                if not (isinstance(p, int) and p == 0):
                    dve.wait_ge(x_lo, 2 * p)
                dve.tensor_scalar(xn[:, :], xall[:, p, :], ln_work[:, 0:1], ln_work[:, 7:8], ALU.subtract,
                                  ALU.mult).then_inc(xn_ready, 1)

            layernorm_stats(0, 0, 0)
            layernorm_apply(0)

            def step(p, i, par, project, combine, residual, last=False, weights=None, drain=False):
                r, r2 = p - 1, p - 2

                def maxima(b, t):
                    n = 8 * p + 4 * b + t
                    dve.wait_ge(t_mm, n + 1)
                    dve.tensor_reduce(qmax[:, t, b, :], dve_ring[t % 2][:, :].rearrange("n (h d) -> n h d", d=DH),
                                      AX.X, ALU.max).then_inc(t_max, 1)
                    dve.wait_ge(k_mm, n + 1)
                    dve.tensor_reduce(kneg[:, k_slot(b, t):k_slot(b, t) + 1], k_ring[t % 2][:, :], AX.X,
                                      ALU.min).then_inc(k_max, 1)

                def normalise(b, t):
                    n = 8 * r + 4 * b + t
                    dve.wait_ge(b_mm, n + 1)
                    e = eq[:, 1 - par, b, t, :]
                    dve.tensor_tensor(e, e, dve_ring[t % 2][:, :], ALU.mult).then_inc(q_norm, 1)

                if project:
                    for t in range(4):
                        maxima(0, t)
                    if not last:
                        layernorm_stats(p + 1, i + par, 1 - par)
                    for t in range(4):
                        maxima(1, t)
                if drain:
                    ffn_input(*((0, 6) if combine else (12, 14)))
                if combine:
                    dve.wait_ge(den_spread, 64 * (r + 1))
                    dve.reciprocal(rden[:, :], den_sq[:, :]).then_inc(rden_step, 1)
                    dve.wait_ge(rden_step, 2 * r + 1)
                    if residual:
                        dve.wait_ge(rden_gathered, 32 * r)
                    dve.tensor_copy(rden_parts[:, 0, :], rden[:, :]).then_inc(rden_step, 1)
                    dve.wait_ge(rden_step, 2 * r + 2)
                    dve.tensor_tensor(rden_parts[:, 1, :], rden[:, :], rden_parts[:, 0, :].bitcast(F32),
                                      ALU.subtract).then_inc(rden_ready, 1)
                if project and not last:
                    layernorm_apply(p + 1)
                if weights:
                    unpack(p, *weights)
                if drain and combine:
                    ffn_input(6, 8)
                if combine:
                    normalise(0, 0)
                    normalise(0, 1)
                if residual:
                    dve.wait_ge(ss_spread, 16 * (r2 + 1))
                    dve.tensor_scalar(ss_max[:, :], ss_sq[:, :], 1e-24, None, ALU.max).then_inc(ss_bounded, 1)
                if combine:
                    normalise(0, 2)
                    dve.wait_ge(m_mm, r + 1)
                    dve.wait_ge(kinv_ready, r + 1)
                    dve.tensor_tensor(fold[:, :, :], small[1][:, :].rearrange("o (s c) -> o s c", c=C),
                                      kinv[:, 1 - par, :].unsqueeze(2).to_broadcast([P, 2 * OT, C]),
                                      ALU.mult).then_inc(m_evac, 1)
                    normalise(0, 3)
                    if drain:
                        ffn_input(8, 9)
                    normalise(1, 0)
                    normalise(1, 1)
                    if drain:
                        ffn_input(9, 10)
                    normalise(1, 2)
                    normalise(1, 3)
                if drain:
                    ffn_input(*((10, 12) if combine else (14, 15)))
                if residual:
                    dve.wait_ge(rn_mm, r2 + 1)
                    dve.wait_ge(y_evac, 2 * (r2 + 1))
                    dve.tensor_tensor(yn[:, :], y0[:, :], small[1][:, :], ALU.mult).then_inc(yn_ready, 1)
                    dve.wait_ge(yn_ready, r2 + 1)
                    dve.scalar_tensor_tensor(out=xall[:, r2, :], in0=yn[:, :], scalar=gate_col[:, 0:1],
                                             in1=xall[:, r2, :], op0=ALU.mult, op1=ALU.add).then_inc(x1_done, 1)
                if project:
                    dve.wait_ge(k_exp, 8 * p + 8)
                    dve.reciprocal(kinv[:, par, :], ksum[:, :]).then_inc(kinv_ready, 1)
                if residual:
                    masks_made(dve)
                    dve.wait_ge(x1_done, r2 + 1)
                    dve.bn_stats(stats2[:, r2, :], xall[:, r2, :]).then_inc(bn2_done, 1)

            def ffn_low(k):
                cols = slice(k * P, (k + 1) * P)
                dve.wait_ge(a_mm, PAIRS)
                dve.wait_ge(xT_hi_ready, k + 1)
                dve.tensor_tensor(xT_lo[:, :, cols], drain_ring[k % 4][:, :].rearrange("k (g r) -> k g r", g=GH),
                                  xT_hi[:, :, cols], ALU.subtract).then_inc(xT_lo_ready, 1)

            def ffn_input(first, end):
                for k in range(first, end):
                    part = [n for n, (start, _) in enumerate(ln2_parts) if k >= start][-1]
                    dve.wait_ge(ln2_step, 9 * part + 9)
                    if k == 0:
                        dve.wait_ge(ct_mm, PAIRS)
                    if k >= 2:
                        dve.wait_ge(xT_mm, k - 1)
                    dve.tensor_scalar(xn2[:, k % 2, :], xall[:, k, :], ln2_work[:, k, 0:1], ln2_work[:, k, 6:7],
                                      ALU.subtract, ALU.mult).then_inc(xn2_ready, 1)
                    if k >= 2:
                        ffn_low(k - 2)

            step(0, 0, 0, True, False, False)
            step(1, 0, 1, True, True, False)
            with dve.Fori(1, GH + 1) as i:
                step(2 * i, i, 0, True, True, True, weights=(0, i - 1, 1))
                step(2 * i + 1, i, 1, True, True, True, weights=(1, i - 1, 1))
            with dve.Fori(GH + 1, PAIRS // 2 - 1) as i:
                step(2 * i, i, 0, True, True, True, weights=(2, DOWNS * i - DOWNS * (GH + 1), 2))
                step(2 * i + 1, i, 1, True, True, True, weights=(2, DOWNS * i - DOWNS * (GH + 1) + 2, 2))
            step(PAIRS - 2, PAIRS // 2 - 1, 0, True, True, True, weights=(2, IT - 3, 2))
            step(PAIRS - 1, PAIRS // 2 - 1, 1, True, True, True, last=True, weights=(2, IT - 1, 1))
            step(PAIRS, PAIRS // 2, 0, False, True, True, drain=True)
            step(PAIRS + 1, PAIRS // 2, 1, False, False, True, drain=True)
            ffn_input(PAIRS - 1, PAIRS)
            ffn_low(PAIRS - 2)
            ffn_low(PAIRS - 1)
            dve.wait_ge(bn2_done, PAIRS)
            dve.wait_ge(w_int, PAIRS - 2)


def feed_forward(nc, xall, w_gu, d_int, xT_hi, xT_lo, scale_T, g_ffn, down_scales, out):
    with ExitStack() as st:
        def sb(name, shape, dt=F32):
            return st.enter_context(nc.sbuf_tensor(name, shape, dt))

        def sem(name):
            return st.enter_context(nc.semaphore(name))

        wd_hi, wd_lo = sb("wd_hi", [P, IT, N], F32R), sb("wd_lo", [P, IT, N], F32R)
        d_scale = sb("d_scale", [P, IT, N], F16)
        wd = sb("wd", [P, 2, N])
        tanh_col = sb("tanh_col2", [P, 1])
        acc = sb("acc", [P, 3, 2, CHUNK])
        sig = sb("sig", [P, CHUNK])
        act_gate = sb("act_gate", [P, CHUNK])
        inter = sb("inter", [P, CHUNK])
        in_hi, in_lo = sb("in_hi", [P, 3, CHUNK], F32R), sb("in_lo", [P, 3, CHUNK], F32R)
        y16 = sb("y16", [P, TPC, N], F16)

        bank = [st.enter_context(nc.psum_tensor(f"ffn_bank{i}", [P, 512], F32)) for i in range(8)]
        y_bank = bank[0:4]
        gu_bank = bank[4:8]

        small_in, d_scale_in, tanh_ready = sem("small_in"), sem("d_scale_in"), sem("tanh_ready")
        d_scaled, d_hi, d_lo = (sem(n) for n in ("d_scaled", "d_hi", "d_lo"))
        gu_mm, s0_done, acc_done, sig_ready, gs_ready, inter_ready, in_hi_ready, in_lo_ready, down_mm = (
            sem(n) for n in ("gu_mm", "s0_done", "acc_done", "sig_ready", "gs_ready", "inter_ready", "in_hi_ready",
                             "in_lo_ready", "down_mm"))
        y16_ready, out_ready, stored = sem("y16_ready"), sem("out_ready"), sem("stored")

        block = st.enter_context(nc.Block())

        def last_unit(j, it, first):
            if it:
                return j, it - 1, first
            return None if first else (j - 1, IT - 1, isinstance(j, int) and j == 1)

        def two_units_back(j, it, first):
            return last_unit(*last_unit(j, it, first))

        def projected(j, it, first=None):
            return (IT - 1 + TPC) * j + (it + 1 if it < IT - 1 else it + TPC)

        @block.sync
        def _(sp):
            sp.dma_start(tanh_col[:, :], g_ffn.rearrange("(c one) -> c one", one=1).to_broadcast([P, 1])).then_inc(small_in, 16)
            sp.dma_start(d_scale[:, :, :].rearrange("p g n -> p (g n)"),
                         down_scales.rearrange("g n -> (g n)").partition_broadcast(P)).then_inc(d_scale_in, 16)
            out_rows = out.rearrange("(p two) c n -> p (two c) n", two=2)
            with sp.Fori(0, PAIRS) as tile:
                sp.wait_ge(out_ready, tile + 1)
                sp.dma_start(out_rows[tile], xall[:, tile, :]).then_inc(stored, 16)
            sp.wait_ge(stored, 16 * PAIRS)

        @block.gpsimd
        def _(pool):
            def low_part(j, it, first):
                n, w = IT * j + it, width(it)
                pool.wait_ge(in_hi_ready, n + 1)
                if not (first and it < 2):
                    pool.wait_ge(down_mm, projected(*two_units_back(j, it, first)))
                pool.tensor_tensor(in_lo[0:w, it % 3, :], inter[0:w, :], in_hi[0:w, it % 3, :].bitcast(F32),
                                   ALU.subtract).then_inc(in_lo_ready, 1)

            for it in range(IT):
                low_part(0, it, True)
            with pool.Fori(1, CHUNKS) as j:
                for it in range(IT):
                    low_part(j, it, False)

        @block.scalar
        def _(act):
            act.wait_ge(small_in, 16)
            act.activation(tanh_col[:, :], tanh_col[:, :], ACT.Tanh).then_inc(tanh_ready, 1)

            def high_down(k):
                act.wait_ge(d_scaled, k + 1)
                act.activation(wd_hi[0:width(k), k, :], wd[0:width(k), k % 2, :], ACT.Copy).then_inc(d_hi, 1)

            def open_sum(j, it, m, first):
                n, w = IT * j + it, width(it)
                act.wait_ge(gu_mm, 8 * n + m + 1)
                if not (first and it < 2):
                    act.wait_ge(inter_ready, n - 1)
                act.activation(acc[0:w, it % 3, m, :], gu_bank[m][0:w, :], ACT.Copy,
                               scale=scale_T[0:w, it, 4 * m:4 * m + 1]).then_inc(s0_done, 1)

            def sigmoid(j, it, first):
                n, w = IT * j + it, width(it)
                act.wait_ge(acc_done, 6 * n + 5)
                if not (first and it == 0):
                    act.wait_ge(gs_ready, n)
                act.activation(sig[0:w, :], acc[0:w, it % 3, 0, :], ACT.Sigmoid).then_inc(sig_ready, 1)

            def high_part(j, it, first):
                n, w = IT * j + it, width(it)
                act.wait_ge(inter_ready, n + 1)
                if not (first and it < 2):
                    act.wait_ge(down_mm, projected(*two_units_back(j, it, first)))
                act.activation(in_hi[0:w, it % 3, :], inter[0:w, :], ACT.Copy).then_inc(in_hi_ready, 1)

            def half_precision(j, t):
                act.wait_ge(down_mm, projected(j, IT - 1) - TPC + t + 1)
                act.activation(y16[:, t, :], y_bank[t][:, :], ACT.Copy).then_inc(y16_ready, 1)

            def chunk(j, first):
                for it in range(IT):
                    before = last_unit(j, it, first)
                    evacuate = not first and it == 1
                    if before:
                        sigmoid(*before)
                    if it == 2 and not first:
                        half_precision(j - 1, 3)
                    open_sum(j, it, 0, first)
                    if evacuate:
                        half_precision(j - 1, 0)
                    open_sum(j, it, 1, first)
                    if evacuate:
                        half_precision(j - 1, 1)
                    if first and it:
                        high_down(it - 1)
                    if before:
                        high_part(*before)
                    if evacuate:
                        half_precision(j - 1, 2)
                    if it == IT - 1 and not first:
                        act.wait_ge(out_ready, TPC * j)

            chunk(0, True)
            high_down(IT - 1)
            with act.Fori(1, CHUNKS) as j:
                chunk(j, False)
            sigmoid(CHUNKS - 1, IT - 1, False)
            high_part(CHUNKS - 1, IT - 1, False)
            for t in range(TPC):
                half_precision(CHUNKS - 1, t)

        @block.tensor
        def _(pe):
            def gate_up(j, it, job, first):
                n, w, (g, m) = IT * j + it, width(it), divmod(job, 2)
                if job < 4:
                    if not (first and it == 0):
                        pe.wait_ge(acc_done, 6 * n - 3 + job)
                elif job < 6:
                    pe.wait_ge(s0_done, 2 * n + job - 3)
                else:
                    pe.wait_ge(acc_done, 6 * n + job - 5)
                lhsT = w_gu[:, m, g, it * P:it * P + w]
                rows = bass.ds(j * CHUNK, CHUNK)
                pe.matmul(gu_bank[job % 4][0:w, :], lhsT, xT_hi[:, g, rows], start=True, stop=False)
                pe.matmul(gu_bank[job % 4][0:w, :], lhsT, xT_lo[:, g, rows], start=False, stop=True).then_inc(gu_mm, 1)

            def down_product(j, it, first, k):
                n, w, buf = IT * j + it, width(it), it % 3
                kind, t = divmod(k, TPC) if it < IT - 1 else (k % 3, k // 3)
                if k == 0:
                    pe.wait_ge(in_hi_ready, n + 1)
                    if first:
                        pe.wait_ge(d_lo, it + 1)
                if it == 0 and not first and kind == 0:
                    pe.wait_ge(y16_ready, TPC * (j - 1) + t + 1)
                if kind == 2 and t == 0:
                    pe.wait_ge(in_lo_ready, n + 1)
                left = (in_hi, in_hi, in_lo)[kind][0:w, buf, t * P:(t + 1) * P]
                right = (wd_hi, wd_lo, wd_hi)[kind][0:w, it, :]
                ins = pe.matmul(y_bank[t][:, :], left, right, start=(it == 0 and kind == 0), stop=(it == IT - 1 and kind == 2))
                if k == 11 or it == IT - 1 and kind == 2:
                    ins.then_inc(down_mm, 1)

            def chunk(j, first):
                for it in range(IT):
                    before = last_unit(j, it, first)
                    before = before and last_unit(*before)
                    k = 0
                    for job in range(8):
                        gate_up(j, it, job, first)
                        while before and k < 12 * (job + 1) // 8:
                            down_product(*before, k)
                            k += 1

            chunk(0, True)
            with pe.Fori(1, CHUNKS) as j:
                chunk(j, False)
            for it in (IT - 2, IT - 1):
                for k in range(12):
                    down_product(CHUNKS - 1, it, False, k)

        @block.vector
        def _(dve):
            def add_group(j, it, job):
                n, w, (g, m) = IT * j + it, width(it), divmod(job, 2)
                dve.wait_ge(gu_mm, 8 * n + job + 1)
                if g == 1:
                    dve.wait_ge(s0_done, 2 * n + m + 1)
                else:
                    dve.wait_ge(acc_done, 6 * n + job - 3)
                dve.scalar_tensor_tensor(out=acc[0:w, it % 3, m, :], in0=gu_bank[job % 4][0:w, :],
                                         scalar=scale_T[0:w, it, 4 * m + g:4 * m + g + 1], in1=acc[0:w, it % 3, m, :],
                                         op0=ALU.mult, op1=ALU.add).then_inc(acc_done, 1)

            def activated(j, it, first):
                n, w, buf = IT * j + it, width(it), it % 3
                dve.wait_ge(sig_ready, n + 1)
                if not (first and it == 0):
                    dve.wait_ge(inter_ready, n)
                dve.tensor_tensor(act_gate[0:w, :], acc[0:w, buf, 0, :], sig[0:w, :], ALU.mult).then_inc(gs_ready, 1)
                dve.wait_ge(gs_ready, n + 1)
                dve.wait_ge(acc_done, 6 * n + 6)
                if not (first and it == 0):
                    dve.wait_ge(in_lo_ready, n)
                dve.tensor_tensor(inter[0:w, :], act_gate[0:w, :], acc[0:w, buf, 1, :],
                                  ALU.mult).then_inc(inter_ready, 1)

            def residual(j, t):
                tile = TPC * j + t
                dve.wait_ge(tanh_ready, 1)
                dve.wait_ge(y16_ready, tile + 1)
                dve.scalar_tensor_tensor(out=xall[:, tile, :], in0=y16[:, t, :], scalar=tanh_col[:, 0:1],
                                         in1=xall[:, tile, :], op0=ALU.mult, op1=ALU.add).then_inc(out_ready, 1)

            def scale_down(k):
                w = width(k)
                if k == 0:
                    dve.wait_ge(d_scale_in, 16)
                else:
                    dve.wait_ge(d_lo, k)
                dve.tensor_tensor(wd[0:w, k % 2, :], d_int[0:w, k, :], d_scale[0:w, k, :], ALU.mult).then_inc(d_scaled, 1)

            def low_down(k):
                w = width(k)
                dve.wait_ge(d_hi, k + 1)
                dve.tensor_tensor(wd_lo[0:w, k, :], wd[0:w, k % 2, :], wd_hi[0:w, k, :].bitcast(F32),
                                  ALU.subtract).then_inc(d_lo, 1)

            def chunk(j, first):
                for it in range(IT):
                    before = last_unit(j, it, first)
                    if before:
                        activated(*before)
                    for job in range(2, 8):
                        add_group(j, it, job)
                        if first and it and job == 4:
                            low_down(it - 1)
                    if first:
                        scale_down(it)
                    if 3 <= it < 3 + TPC and not first:
                        residual(j - 1, it - 3)

            chunk(0, True)
            low_down(IT - 1)
            with dve.Fori(1, CHUNKS) as j:
                chunk(j, False)
            activated(CHUNKS - 1, IT - 1, False)
            for t in range(TPC):
                residual(CHUNKS - 1, t)


_INS = ["x", "ctx_4096", "g_xattn", "g_ffn", "L0_xattn_Wq", "L0_xattn_Wk", "L0_xattn_Wv", "L0_xattn_Wo", "L0_xattn_bo",
        "L0_xattn_g", "L0_ffn_gate_qweight", "L0_ffn_gate_scales", "L0_ffn_gate_zeros", "L0_ffn_up_qweight",
        "L0_ffn_up_scales", "L0_ffn_up_zeros", "L0_ffn_down_qweight", "L0_ffn_down_scales", "L0_ffn_down_zeros"]


def build(nc, x, ctx, g_xattn, g_ffn, wq, wk, wv, wo, bo, g, gate_q, gate_s, gate_z, up_q, up_s, up_z, down_q, down_s,
          down_z, out):
    with ExitStack() as st:
        xall = st.enter_context(nc.sbuf_tensor("xall", [P, PAIRS, N], F32))
        stats2 = st.enter_context(nc.sbuf_tensor("stats2", [P, PAIRS, 6], F32))
        ident = st.enter_context(nc.sbuf_tensor("ident", [P, P], F32))
        w_gu = st.enter_context(nc.sbuf_tensor("w_gu", [P, 2, GH, INTER], BF16))
        d_int = st.enter_context(nc.sbuf_tensor("d_int", [P, IT, N], BF16))
        ek = st.enter_context(nc.sbuf_tensor("ek", [P, 2, OT, N], F32))
        ekT = st.enter_context(nc.sbuf_tensor("ekT", [P, 2, NT, O], F32))
        xT_hi, xT_lo = (t[:, :, :, :].rearrange("p a b c -> p (a b c)").bitcast(F16).rearrange("p (g r) -> p g r", g=GH)
                        for t in (ek, ekT))
        scale_T = st.enter_context(nc.sbuf_tensor("scale_T", [P, IT, 2 * GH], F32))
        gate, up, down = (gate_q, gate_s, gate_z), (up_q, up_s, up_z), (down_q, down_s, down_z)
        attention(nc, x, ctx, g_xattn, wq, wk, wv, wo, bo, g, (gate, up, down), xall, stats2, ident, w_gu, d_int,
                  ek, ekT, xT_hi, xT_lo, scale_T)
        feed_forward(nc, xall, w_gu, d_int, xT_hi, xT_lo, scale_T, g_ffn, down[1], out)


def kernel(**inputs):
    import numpy as np
    import concourse.bacc as bacc
    from concourse.bass_utils import run_bass_kernel_spmd

    nc = bacc.Bacc("TRN2", target_bir_lowering=False, num_devices=1)
    arrays, args = {}, []
    for name in _INS:
        a = np.ascontiguousarray(inputs[name])
        arrays[f"in_{name}"] = a
        args.append(nc.dram_tensor(f"in_{name}", a.shape, mybir.dt.from_np(a.dtype), kind="ExternalInput").ap())
    out = nc.dram_tensor("out_x", (BATCH, C, N), F32, kind="ExternalOutput").ap()
    build(nc, *args, out)
    return run_bass_kernel_spmd(nc, [arrays], core_ids=[0]).results[0]["out_x"]
```
